# Optimizing a Trainium2 kernel written in Bass

```python
import numpy as np
import jax
import jax.numpy as jnp

def _softmax(x, axis=-1):
    return jax.nn.softmax(x, axis=axis)

def _gelu(x):
    return jax.nn.gelu(x, approximate=True)

def _silu(x):
    return jax.nn.silu(x)

def _sigmoid(x):
    return jax.nn.sigmoid(x)

def _layernorm(x, axis=-1, eps=1e-05):
    m = jnp.mean(x, axis=axis, keepdims=True)
    v = jnp.var(x, axis=axis, keepdims=True)
    return (x - m) / jnp.sqrt(v + eps)

def _scatter_add(tgt, idx, src, axis=0):
    return tgt.at[idx].add(src)

def _segment_sum(src, seg, n):
    return jax.ops.segment_sum(src, seg, n)
kernel_name = 'mk_prb_d1_jaxref_r8_6924f2'

def setup_inputs(seed: int=0):
    np.random.seed(seed)
    _w = jnp.asarray

    def _L0_attn_setup():
        import jax, jax.numpy as jnp
        import numpy as np
        HIDDEN = 512
        N_HEADS = 32
        KV_HEADS = 8
        HEAD_DIM = 128
        LOW_RANK = 64
        TOP_K_ROPE = 32
        ROPE_THETA = 10000.0
        B, S = (2, 256)
        GROUPS = N_HEADS // KV_HEADS
        _half = HEAD_DIM // 2
        _m = np.ones(_half, dtype=bool)
        _m[:TOP_K_ROPE] = False
        _m = np.concatenate([_m, _m])
        NOPE_MASK = np.tile(_m, KV_HEADS)
        ROPE_IDX = jnp.asarray(np.where(~NOPE_MASK)[0])
        NOPE_IDX = jnp.asarray(np.where(NOPE_MASK)[0])
        R_DIM = int((~NOPE_MASK).sum())
        C_DIM = LOW_RANK * KV_HEADS

        def _rope_tables(seq_len, dtype):
            inv_freq = 1.0 / ROPE_THETA ** (np.arange(0, HEAD_DIM, 2, dtype=np.float32) / HEAD_DIM)
            pos = np.arange(seq_len, dtype=np.float32)
            freqs = np.outer(pos, inv_freq)
            emb = np.concatenate([freqs, freqs], axis=-1)
            return (jnp.asarray(np.cos(emb), dtype), jnp.asarray(np.sin(emb), dtype))

        def _rotate_half(x):
            x1, x2 = (x[..., :HEAD_DIM // 2], x[..., HEAD_DIM // 2:])
            return jnp.concatenate([-x2, x1], axis=-1)
        key = jax.random.key(seed)
        ks = jax.random.split(key, 7)
        s = 0.02
        return {'hidden_states': jax.random.normal(ks[0], (B, S, HIDDEN), jnp.float32), 'Wq': jax.random.normal(ks[1], (N_HEADS * HEAD_DIM, HIDDEN), jnp.float32) * s, 'Wkr': jax.random.normal(ks[2], (R_DIM, HIDDEN), jnp.float32) * s, 'Wdk': jax.random.normal(ks[3], (C_DIM, HIDDEN), jnp.float32) * s, 'Wupk': jax.random.normal(ks[4], (KV_HEADS * HEAD_DIM - R_DIM, C_DIM), jnp.float32) * s, 'Wupv': jax.random.normal(ks[5], (KV_HEADS * HEAD_DIM, C_DIM), jnp.float32) * s, 'Wo': jax.random.normal(ks[6], (HIDDEN, N_HEADS * HEAD_DIM), jnp.float32) * s}
    _L0_attn_in = _L0_attn_setup()

    def _L0_ffn_setup():
        import jax, jax.numpy as jnp
        import numpy as np
        HD, M = (512, 1792)
        key = jax.random.key(seed)
        k_x, k_g, k_u, k_d = jax.random.split(key, 4)
        scale = 1.0 / np.sqrt(HD)
        x = jax.random.normal(k_x, (4, 256, HD), dtype=jnp.float16)
        W_gate = jax.random.normal(k_g, (M, HD), dtype=jnp.float16) * jnp.float16(scale)
        W_up = jax.random.normal(k_u, (M, HD), dtype=jnp.float16) * jnp.float16(scale)
        W_down = jax.random.normal(k_d, (HD, M), dtype=jnp.float16) * jnp.float16(1.0 / np.sqrt(M))
        return {'x': x, 'W_gate': W_gate, 'W_up': W_up, 'W_down': W_down}
    _L0_ffn_in = _L0_ffn_setup()
    _d = {'L0_attn_hidden_states': _L0_attn_in['hidden_states'], 'L0_attn_Wq': _L0_attn_in['Wq'], 'L0_attn_Wkr': _L0_attn_in['Wkr'], 'L0_attn_Wdk': _L0_attn_in['Wdk'], 'L0_attn_Wupk': _L0_attn_in['Wupk'], 'L0_attn_Wupv': _L0_attn_in['Wupv'], 'L0_attn_Wo': _L0_attn_in['Wo'], 'L0_ffn_W_gate': _L0_ffn_in['W_gate'], 'L0_ffn_W_up': _L0_ffn_in['W_up'], 'L0_ffn_W_down': _L0_ffn_in['W_down']}
    _x0 = _d['L0_attn_hidden_states']
    _d['L0_attn_hidden_states'] = jax.random.normal(jax.random.fold_in(jax.random.key(seed), 1), (2, 1024, 512), dtype=_x0.dtype)
    del _x0
    return _d

def reference(L0_attn_hidden_states, L0_attn_Wq, L0_attn_Wkr, L0_attn_Wdk, L0_attn_Wupk, L0_attn_Wupv, L0_attn_Wo, L0_ffn_W_gate, L0_ffn_W_up, L0_ffn_W_down):

    def _L0_attn_ref(hidden_states, Wq, Wkr, Wdk, Wupk, Wupv, Wo):
        import jax, jax.numpy as jnp
        import numpy as np
        HIDDEN = 512
        N_HEADS = 32
        KV_HEADS = 8
        HEAD_DIM = 128
        LOW_RANK = 64
        TOP_K_ROPE = 32
        ROPE_THETA = 10000.0
        B, S = (2, 256)
        GROUPS = N_HEADS // KV_HEADS
        _half = HEAD_DIM // 2
        _m = np.ones(_half, dtype=bool)
        _m[:TOP_K_ROPE] = False
        _m = np.concatenate([_m, _m])
        NOPE_MASK = np.tile(_m, KV_HEADS)
        ROPE_IDX = jnp.asarray(np.where(~NOPE_MASK)[0])
        NOPE_IDX = jnp.asarray(np.where(NOPE_MASK)[0])
        R_DIM = int((~NOPE_MASK).sum())
        C_DIM = LOW_RANK * KV_HEADS

        def _rope_tables(seq_len, dtype):
            inv_freq = 1.0 / ROPE_THETA ** (np.arange(0, HEAD_DIM, 2, dtype=np.float32) / HEAD_DIM)
            pos = np.arange(seq_len, dtype=np.float32)
            freqs = np.outer(pos, inv_freq)
            emb = np.concatenate([freqs, freqs], axis=-1)
            return (jnp.asarray(np.cos(emb), dtype), jnp.asarray(np.sin(emb), dtype))

        def _rotate_half(x):
            x1, x2 = (x[..., :HEAD_DIM // 2], x[..., HEAD_DIM // 2:])
            return jnp.concatenate([-x2, x1], axis=-1)
        bsz, q_len, _ = hidden_states.shape
        dt = hidden_states.dtype
        q = (hidden_states @ Wq.T).reshape(bsz, q_len, N_HEADS, HEAD_DIM).transpose(0, 2, 1, 3)
        k_r0 = hidden_states @ Wkr.T
        key_flat = jnp.zeros((bsz, q_len, KV_HEADS * HEAD_DIM), dt).at[..., ROPE_IDX].set(k_r0)
        k = key_flat.reshape(bsz, q_len, KV_HEADS, HEAD_DIM).transpose(0, 2, 1, 3)
        cos, sin = _rope_tables(q_len, dt)
        cos, sin = (cos[None, None], sin[None, None])
        q = q * cos + _rotate_half(q) * sin
        k = k * cos + _rotate_half(k) * sin
        k_r = k.transpose(0, 2, 1, 3).reshape(bsz, q_len, KV_HEADS * HEAD_DIM)[..., ROPE_IDX]
        c_kv = hidden_states @ Wdk.T
        k_c = c_kv @ Wupk.T
        v = (c_kv @ Wupv.T).reshape(bsz, q_len, KV_HEADS, HEAD_DIM).transpose(0, 2, 1, 3)
        key_full = jnp.zeros((bsz, q_len, KV_HEADS * HEAD_DIM), dt).at[..., NOPE_IDX].set(k_c).at[..., ROPE_IDX].set(k_r)
        k = key_full.reshape(bsz, q_len, KV_HEADS, HEAD_DIM).transpose(0, 2, 1, 3)
        k = jnp.repeat(k, GROUPS, axis=1)
        v = jnp.repeat(v, GROUPS, axis=1)
        scale = 1.0 / jnp.sqrt(jnp.asarray(HEAD_DIM, dt))
        scores = jnp.einsum('bhqd,bhkd->bhqk', q, k) * scale
        causal = jnp.tril(jnp.ones((q_len, q_len), bool))
        scores = jnp.where(causal[None, None], scores, jnp.asarray(-1000000000.0, dt))
        attn = jax.nn.softmax(scores, axis=-1)
        out = jnp.einsum('bhqk,bhkd->bhqd', attn, v)
        out = out.transpose(0, 2, 1, 3).reshape(bsz, q_len, N_HEADS * HEAD_DIM)
        return out @ Wo.T

    def _L0_ffn_ref(x, W_gate, W_up, W_down):
        import jax, jax.numpy as jnp
        import numpy as np
        HD, M = (512, 1792)
        gate = jnp.einsum('bsh,mh->bsm', x, W_gate)
        up = jnp.einsum('bsh,mh->bsm', x, W_up)
        h = jax.nn.silu(gate) * up
        out = jnp.einsum('bsm,hm->bsh', h, W_down)
        return out
    x = L0_attn_hidden_states
    xn = _layernorm(x, axis=-1)
    x = x + _L0_attn_ref(xn, L0_attn_Wq, L0_attn_Wkr, L0_attn_Wdk, L0_attn_Wupk, L0_attn_Wupv, L0_attn_Wo) + _L0_ffn_ref(xn, L0_ffn_W_gate, L0_ffn_W_up, L0_ffn_W_down)
    return x

_drawn_inputs = setup_inputs


def setup_inputs(seed=0):
    import zlib

    import numpy as np

    out = dict(_drawn_inputs(seed))
    spreads = {}
    factors = {'L0_attn_Wq': 8.0,
     'L0_attn_Wkr': 8.0,
     'L0_attn_Wdk': 2.942,
     'L0_attn_Wupk': 8.0,
     'L0_attn_Wupv': 2.892,
     'L0_attn_Wo': 2.928}
    for name, (base, spread) in spreads.items():
        noise = np.random.default_rng([zlib.crc32(name.encode()), seed]).standard_normal(out[name].shape)
        drawn = base * np.exp(spread * noise) if base else spread * noise
        out[name] = jnp.asarray(drawn.astype(out[name].dtype))
    for name, factor in factors.items():
        out[name] = (out[name] * factor).astype(out[name].dtype)
    return out
```

```python
from contextlib import ExitStack

import concourse.bass as bass
from concourse import mybir

F32 = mybir.dt.float32
F32R = mybir.dt.float32r
F16 = mybir.dt.float16
BF16 = mybir.dt.bfloat16
ACT = mybir.ActivationFunctionType
ALU = mybir.AluOpType
AX = mybir.AxisListType

HI, LO = 0, 1
PASSES = ((HI, HI), (HI, LO), (LO, HI))

P = 128
B, S, D = 2, 1024, 512
HEADS, KVH, DH = 32, 8, 128
GRP = HEADS // KVH
HALF = DH // 2
RH = 32
KC = D // P
C = 512
CC = C // P
M = 1792
MB = M // P
TB = S // P
CHUNK = 512
CT = CHUNK // P
CHUNKS = B * S // CHUNK
FFW = 3 * C
EPS = 1e-5
MASKED = -1e30

RING = 4
G_XT = 0
G_KR = G_XT + KC
G_CT = G_KR + CT
G_KRT = G_CT + CC
G_KN = G_KRT + KVH // 2
G_V = G_KN + KVH // 2
GROUPS = G_V + 2 * CT
STORED = range(G_KRT, GROUPS)
SPLITS = GROUPS - CT


def split_no(n):
    return n + 1 if n < G_KR else n + 1 - CT


def stores_upto(slot, n):
    return sum(4 if m < G_V else 2 for m in STORED if m % RING == slot and m <= n)


PAIRS = KVH // 2
UNITS = 2 * TB
HPB = UNITS * GRP


def unit_kv(n):
    return n // TB


def unit_block(n):
    return n % TB if n < TB else TB - 1 - n % TB


def key_blocks(n):
    return unit_block(n) + 1


def first_key_block(n):
    return sum(key_blocks(m) for m in range(n))


KEYB = first_key_block(UNITS)


def body_schedule():
    out = [("Q", 0, 0), ("QT", 0, 0)]
    for k in range(UNITS + 2):
        tail = []
        if 1 <= k <= UNITS:
            n, J, lag = k - 1, key_blocks(k - 1), 2
            for j in range(J + lag):
                if j < J:
                    tail.append(("T", n, j))
                if j >= lag:
                    tail.append(("PV", n, j - lag))
        parts = [tail[len(tail) * a // 3:len(tail) * (a + 1) // 3] for a in range(3)]
        heads = [[("S", k, h)] if k < UNITS else [] for h in range(GRP)]
        out += heads[0]
        if k + 1 < UNITS:
            out.append(("Q", k + 1, 0))
        out += heads[1]
        if k >= 2:
            out.append(("W", k - 2, 0))
        out += parts[0] + heads[2] + parts[1] + heads[3]
        if k + 1 < UNITS:
            out.append(("QT", k + 1, 0))
        out += parts[2]
    return out


SCHEDULE = body_schedule()
MISC = [e for e in SCHEDULE if e[0] in ("Q", "QT", "W")]
MISC_NO = {e: i for i, e in enumerate(MISC)}


def with_later(name, by):
    out, held = [], []
    for e in SCHEDULE:
        while held and (held[0][0] == 0 or (e[0] == "T" and held[0][1][1] == e[1])):
            out.append(held.pop(0)[1])
        out.append(e)
        for x in held:
            x[0] -= 1
        if e[0] == "S":
            held.append([by, (name, e[1], e[2])])
    return out + [e for _, e in held]


def key_value_and_ffn(nc, a, scr, prime):
    with ExitStack() as ctx:
        def sb(name, shape, dt=F32):
            return ctx.enter_context(nc.sbuf_tensor(name, shape, dt))

        def bank(name):
            return ctx.enter_context(nc.psum_tensor(name, [P, 512], F32))

        def sem(name):
            return ctx.enter_context(nc.semaphore(name))

        ident = sb("ident1", [P, P])
        w_raw = sb("w_raw", [P, 4, 512])
        wdk = sb("wdk", [P, 2, KC, C], F32R)
        wkr = sb("wkr", [P, 2, KC, 512], F32R)
        wupk = sb("wupk", [P, 2, CC, 512], F32R)
        wupv = sb("wupv", [P, 2, 2, CC, 512], F32R)
        ktab = sb("ktab", [P, CT, 2, RH])
        x_in = sb("x_in", [P, CT, D])
        xn = sb("xn", [P, CT, D])
        stats = sb("stats", [P, CT, 6])
        mv = sb("mv", [P, CT, 2])
        var_eps = sb("var_eps", [P, CT])
        power = sb("power", [P, CT])
        rstd = sb("rstd", [P, CT])
        xT = sb("xT1", [P, 2, KC, CHUNK], F32R)
        cT = sb("cT", [P, 2, CC, CHUNK], F32R)
        k_cos = sb("k_cos", [P, 512])
        k_sin = sb("k_sin", [P, 512])
        k_rot = sb("k_rot", [P, CT, 512])
        stage = sb("stage", [P, RING, 2, 512], F32R)
        ff_raw = sb("ff_raw", [P, 2, FFW], F16)
        ff_w = sb("ff_w", [P, 2, FFW], F32R)
        silu = sb("silu", [P, 512])
        h32 = sb("h32", [P, 512])
        hT = sb("hT", [P, 2, 2, 512], F32R)
        ff_out = sb("ff_out", [P, 2, D])
        ring = [bank(f"ring{i}") for i in range(RING)]
        down = [bank(f"down{i}") for i in range(CT)]

        ident_ready = sem("ident_ready")
        w_loaded = sem("w_loaded")
        w_hi = sem("w_hi")
        w_split = sem("w_split")
        x_loaded = sem("x_loaded")
        tab_loaded = sem("tab_loaded")
        ln_step = sem("ln_step")
        rstd_ready = sem("rstd_ready")
        xn_ready = sem("xn_ready")
        group_done = sem("group_done")
        hi_ready = sem("hi_ready")
        emptied = sem("emptied")
        rotated = sem("rotated")
        stored = [sem(f"stored{i}") for i in range(RING)]
        xT_stored = sem("xT_stored")
        ff_loaded = [sem(f"ff_loaded{i}") for i in range(2)]
        ff_cast = sem("ff_cast")
        gate_done = sem("gate_done")
        up_done = sem("up_done")
        silu_ready = sem("silu_ready")
        h_ready = sem("h_ready")
        h_hi = sem("h_hi")
        h_split = sem("h_split")
        down_done = sem("down_done")
        ff_copied = sem("ff_copied")
        ff_stored = [sem(f"ff_stored{i}") for i in range(2)]

        prime += [(group_done, GROUPS), (hi_ready, SPLITS), (emptied, GROUPS), (rotated, CT),
                  (xn_ready, CT), (xT_stored, 32), (ff_cast, MB), (gate_done, MB),
                  (up_done, MB), (silu_ready, MB), (h_ready, MB), (h_hi, MB), (h_split, MB),
                  (down_done, MB), (ff_copied, CT), (x_loaded, 16), (tab_loaded, 16),
                  (ff_loaded[0], 16 * MB // 2), (ff_loaded[1], 16 * MB // 2),
                  (ff_stored[0], 16 * CT // 2), (ff_stored[1], 16 * CT // 2),
                  (ln_step, 2), (rstd_ready, 1)]
        prime += [(stored[s], 16 * stores_upto(s, GROUPS)) for s in range(RING)]
        with nc.Block() as start:
            @start.sync
            def _(sp):
                for s, n in prime:
                    sp.sem_inc(s, n)

        weights = [(a["wdk"], wdk), (a["wkr"], wkr), (a["wupk"], wupk)]
        weights = [(src, dst[:, HI], dst[:, LO]) for src, dst in weights]
        weights += [(a["wupv"][v], wupv[:, HI, v], wupv[:, LO, v]) for v in range(2)]
        block = ctx.enter_context(nc.Block())

        @block.sync
        def _(sp):
            for n, (src, _, _) in enumerate(weights):
                if n:
                    sp.wait_ge(w_split, n)
                sp.dma_start(w_raw[:], src).then_inc(w_loaded, 16)
            with sp.Fori(0, B) as b:
                with sp.Fori(0, S // CHUNK) as half:
                    c1 = b * (S // CHUNK) + half + 1
                    sp.wait_ge(xn_ready, c1 * CT)
                    sp.dma_start(x_in[:], a["x"][b, half]).then_inc(x_loaded, 16)
                    sp.wait_ge(emptied, c1 * GROUPS - GROUPS + G_CT)
                    sp.dma_start(ktab[:], a["ktab"][half]).then_inc(tab_loaded, 16)
                    sp.wait_ge(emptied, c1 * GROUPS + G_KR)
                    for part in (HI, LO):
                        sp.dma_start(scr["xT"][b, :, part, :, bass.ds(half * CHUNK, CHUNK)],
                                     xT[:, part].bitcast(F32)).then_inc(xT_stored, 16)
                    for n in STORED:
                        s = n % RING
                        sp.wait_ge(emptied, c1 * GROUPS + n + 1)
                        if n < G_V:
                            pair, low = (n - G_KRT, 0) if n < G_KN else (n - G_KN, RH)
                            for q in range(4):
                                row = (q % 2) * HALF + low
                                sp.dma_start(scr["k"][b, 2 * pair + q // 2, row:row + RH, :,
                                                      bass.ds(half * CHUNK, CHUNK)],
                                             stage[q * RH:(q + 1) * RH, s].bitcast(F32))\
                                    .then_inc(stored[s], 16)
                        else:
                            t, v = (n - G_V) // 2, (n - G_V) % 2
                            for part in (HI, LO):
                                sp.dma_start(
                                    scr["v"][b, v * 4:v * 4 + 4, :, part, half * CT + t, :]
                                    .rearrange("g p d -> p g d"),
                                    stage[:, s, part].bitcast(F32).rearrange("p (g d) -> p g d", g=4))\
                                    .then_inc(stored[s], 16)
                    with sp.Fori(0, MB // 2) as m2:
                        for o in range(2):
                            sp.wait_ge(ff_cast, c1 * MB + m2 * 2 + (o - 1))
                            sp.dma_start(ff_raw[:, o], a["ffw"][m2 * 2 + o]).then_inc(ff_loaded[o], 16)
            sp.wait_ge(xT_stored, 32 * (CHUNKS + 1))
            for s in range(RING):
                sp.wait_ge(stored[s], 16 * stores_upto(s, GROUPS) * (CHUNKS + 1))
            for o in range(2):
                sp.wait_ge(ff_stored[o], 16 * (CT // 2) * (CHUNKS + 1))

        @block.gpsimd
        def _(pool):
            nc.gpsimd.memset(power[:], -0.5).then_inc(ident_ready, 1)
            nc.gpsimd.memset(ident[:], 0.0).then_inc(ident_ready, 1)
            pool.wait_ge(ident_ready, 2)
            nc.gpsimd.affine_select(out=ident[:], in_=ident[:], compare_op=ALU.not_equal, fill=1.0,
                                    base=0, pattern=[[-1, P]], channel_multiplier=1)\
                .then_inc(ident_ready, 1)
            with pool.Fori(0, CHUNKS) as c:
                c1 = c + 1
                pool.wait_ge(ln_step, c1 * 2 + 2)
                nc.gpsimd.tensor_tensor(rstd[:], var_eps[:], power[:], ALU.pow).then_inc(rstd_ready, 1)
                for t in range(CT):
                    kc, ks, kr = (v.rearrange("p (g h r) -> p g h r", h=2, r=RH)
                                  for v in (k_cos[:], k_sin[:], k_rot[:, t]))
                    pool.wait_ge(emptied, c1 * GROUPS + G_KR + t + 1)
                    nc.gpsimd.tensor_tensor(kr[:, :, 0], kc[:, :, 0], ks[:, :, 0], ALU.subtract)
                    nc.gpsimd.tensor_tensor(kr[:, :, 1], kc[:, :, 1], ks[:, :, 1], ALU.add)\
                        .then_inc(rotated, 1)

        @block.scalar
        def _(act):
            for n, (_, hi, _) in enumerate(weights):
                act.wait_ge(w_loaded, 16 * (n + 1))
                nc.scalar.activation(hi, w_raw[:], ACT.Copy).then_inc(w_hi, 1)

            def cast(c1, m, o):
                act.wait_ge(ff_loaded[o], (c1 * MB + m + (2 - o)) * 8)
                act.wait_ge(down_done, c1 * MB + m - 1)
                nc.scalar.activation(ff_w[:, o], ff_raw[:, o], ACT.Copy).then_inc(ff_cast, 1)

            def gate(c1, m, o):
                act.wait_ge(gate_done, c1 * MB + m + 1)
                act.wait_ge(h_ready, c1 * MB + m)
                nc.scalar.activation(silu[:], ring[o][:], ACT.Silu).then_inc(silu_ready, 1)
                act.wait_ge(h_ready, c1 * MB + m + 1)
                act.wait_ge(down_done, c1 * MB + m - 1)
                nc.scalar.activation(hT[:, o, HI], h32[:], ACT.Copy).then_inc(h_hi, 1)

            with act.Fori(0, B) as b:
                with act.Fori(0, S // CHUNK) as half:
                    c1 = b * (S // CHUNK) + half + 1
                    for n in list(range(G_XT, G_KR)) + list(range(G_CT, GROUPS)):
                        act.wait_ge(group_done, c1 * GROUPS + n + 1)
                        if n < G_KR:
                            if n == 0:
                                act.wait_ge(xT_stored, c1 * 32)
                            dst = xT[:, HI, n - G_XT]
                        elif n < G_KRT:
                            dst = cT[:, HI, n - G_CT]
                        else:
                            s = n % RING
                            act.wait_ge(stored[s], c1 * (16 * stores_upto(s, GROUPS)) + 16 * stores_upto(s, n - 1))
                            dst = stage[:, s, HI]
                        nc.scalar.activation(dst, ring[n % RING][:], ACT.Copy).then_inc(hi_ready, 1)
                    cast(c1, 0, 0)
                    cast(c1, 1, 1)
                    with act.Fori(0, MB // 2 - 1) as m2:
                        for o in range(2):
                            gate(c1, m2 * 2 + o, o)
                            cast(c1, m2 * 2 + (o + 2), o)
                    for o in range(2):
                        gate(c1, MB - 2 + o, o)
                    for t in range(CT):
                        if t == 0:
                            act.wait_ge(down_done, c1 * MB + MB)
                        act.wait_ge(ff_stored[t % 2], (c1 * (CT // 2) + t // 2) * 16)
                        nc.scalar.activation(ff_out[:, t % 2], down[t][:], ACT.Copy).then_inc(ff_copied, 1)
                        act.wait_ge(ff_copied, c1 * CT + t + 1)
                        act.dma_start(scr["ffn"][b, :, half * CT + t, :], ff_out[:, t % 2])\
                            .then_inc(ff_stored[t % 2], 16)

        @block.vector
        def _(dve):
            for n, (_, hi, lo) in enumerate(weights):
                dve.wait_ge(w_hi, n + 1)
                nc.vector.tensor_tensor(lo, w_raw[:], hi.bitcast(F32), ALU.subtract).then_inc(w_split, 1)

            def split_lo(c1, n, hi, lo):
                dve.wait_ge(hi_ready, c1 * SPLITS + split_no(n))
                nc.vector.tensor_tensor(lo, ring[n % RING][:], hi.bitcast(F32), ALU.subtract)\
                    .then_inc(emptied, 1)

            def hidden(c1, m, o):
                dve.wait_ge(up_done, c1 * MB + m + 1)
                dve.wait_ge(silu_ready, c1 * MB + m + 1)
                dve.wait_ge(h_split, c1 * MB + m)
                nc.vector.tensor_tensor(h32[:], ring[2 + o][:], silu[:], ALU.mult).then_inc(h_ready, 1)
                dve.wait_ge(h_hi, c1 * MB + m + 1)
                nc.vector.tensor_tensor(hT[:, o, LO], h32[:], hT[:, o, HI].bitcast(F32), ALU.subtract)\
                    .then_inc(h_split, 1)

            with dve.Fori(0, CHUNKS) as c:
                c1 = c + 1
                dve.wait_ge(x_loaded, c1 * 16 + 16)
                for t in range(CT):
                    nc.vector.bn_stats(stats[:, t], x_in[:, t])
                dve.drain()
                for t in range(CT):
                    ins = nc.vector.bn_aggr(mv[:, t], stats[:, t])
                ins.then_inc(ln_step, 1)
                dve.wait_ge(ln_step, c1 * 2 + 1)
                nc.vector.tensor_scalar(var_eps[:], mv[:, :, 1], EPS, None, ALU.add).then_inc(ln_step, 1)
                dve.wait_ge(rstd_ready, c1 + 1)
                for t in range(CT):
                    nc.vector.tensor_scalar(xn[:, t], x_in[:, t], mv[:, t, 0:1], rstd[:, t:t + 1],
                                            ALU.subtract, ALU.mult).then_inc(xn_ready, 1)
                for n in range(G_XT, G_KR):
                    split_lo(c1, n, xT[:, HI, n - G_XT], xT[:, LO, n - G_XT])
                dve.wait_ge(tab_loaded, c1 * 16 + 16)
                for t in range(CT):
                    n = G_KR + t
                    k, kc, ks = (v.rearrange("p (g h r) -> p g h r", h=2, r=RH)
                                 for v in (ring[n % RING][:], k_cos[:], k_sin[:]))
                    cos, sin = (ktab[:, t, i].unsqueeze(1).broadcast_to([P, KVH, RH]) for i in range(2))
                    dve.wait_ge(group_done, c1 * GROUPS + n + 1)
                    dve.wait_ge(rotated, c1 * CT + t)
                    for h in range(2):
                        nc.vector.tensor_tensor(kc[:, :, h], k[:, :, h], cos, ALU.mult)
                    nc.vector.tensor_tensor(ks[:, :, 0], k[:, :, 1], sin, ALU.mult)
                    nc.vector.tensor_tensor(ks[:, :, 1], k[:, :, 0], sin, ALU.mult).then_inc(emptied, 1)
                for n in range(G_CT, GROUPS):
                    dst = cT[:, :, n - G_CT] if n < G_KRT else stage[:, n % RING]
                    split_lo(c1, n, dst[:, HI], dst[:, LO])
                with dve.Fori(0, MB // 2) as m2:
                    for o in range(2):
                        hidden(c1, m2 * 2 + o, o)

        @block.tensor
        def _(pe):
            def products(n, c1, pairs, out=None):
                pe.wait_ge(emptied, c1 * GROUPS + n + 1 - RING)
                for i, (l, r) in enumerate(pairs):
                    mm = nc.tensor.matmul(ring[n % RING][:], l, r, start=(i == 0), stop=(i == len(pairs) - 1))
                mm.then_inc(group_done, 1)

            def transposes(n, c1, blocks):
                pe.wait_ge(emptied, c1 * GROUPS + n + 1 - RING)
                for i, src in enumerate(blocks):
                    mm = nc.tensor.transpose(ring[n % RING][:, i * P:(i + 1) * P], src, ident[:])
                mm.then_inc(group_done, 1)

            def gate_up(c1, m, o):
                pe.wait_ge(ff_cast, c1 * MB + m + 1)
                pe.wait_ge(h_ready, c1 * MB + m - 1)
                for side, done in ((0, gate_done), (1, up_done)):
                    w = ff_w[:, o, side * C:(side + 1) * C]
                    for i in range(2 * KC):
                        mm = nc.tensor.matmul(ring[2 * side + o][:], w[:, (i // 2) * P:(i // 2 + 1) * P],
                                              xT[:, i % 2, i // 2], start=(i == 0), stop=(i == 2 * KC - 1))
                    mm.then_inc(done, 1)

            def project_down(c1, m, o, first=False, last=False):
                pe.wait_ge(h_split, c1 * MB + m + 1)
                for t in range(CT):
                    for part in (HI, LO):
                        mm = nc.tensor.matmul(down[t][:], hT[:, o, part, t * P:(t + 1) * P],
                                              ff_w[:, o, 2 * C:3 * C],
                                              start=(first and part == HI), stop=(last and part == LO))
                mm.then_inc(down_done, 1)

            pe.wait_ge(ident_ready, 3)
            with pe.Fori(0, CHUNKS) as c:
                c1 = c + 1
                pe.wait_ge(xn_ready, c1 * CT + CT)
                pe.wait_ge(h_ready, c1 * MB)
                for k in range(KC):
                    transposes(G_XT + k, c1, [xn[:, t, k * P:(k + 1) * P] for t in range(CT)])
                pe.wait_ge(emptied, c1 * GROUPS + G_KR)
                pe.wait_ge(w_split, len(weights))
                for t in range(CT):
                    products(G_KR + t, c1, [(xT[:, x, k, t * P:(t + 1) * P], wkr[:, w, k])
                                            for k in range(KC) for x, w in PASSES])
                for m in range(CC):
                    products(G_CT + m, c1, [(wdk[:, w, k, m * P:(m + 1) * P], xT[:, x, k])
                                            for k in range(KC) for w, x in PASSES])
                pe.wait_ge(rotated, c1 * CT + CT)
                for q in range(KVH // 2):
                    transposes(G_KRT + q, c1, [k_rot[:, t, q * P:(q + 1) * P] for t in range(CT)])
                pe.wait_ge(emptied, c1 * GROUPS + G_KRT)
                for q in range(KVH // 2):
                    products(G_KN + q, c1, [(wupk[:, w, k, q * P:(q + 1) * P], cT[:, x, k])
                                            for k in range(CC) for w, x in PASSES])
                for t in range(CT):
                    for v in range(2):
                        products(G_V + 2 * t + v, c1, [(cT[:, x, k, t * P:(t + 1) * P], wupv[:, w, v, k])
                                                       for k in range(CC) for x, w in PASSES])
                pe.wait_ge(emptied, c1 * GROUPS + GROUPS)
                gate_up(c1, 0, 0)
                gate_up(c1, 1, 1)
                pe.wait_ge(ff_copied, c1 * CT)
                project_down(c1, 0, 0, first=True)
                with pe.Fori(0, MB // 2 - 1) as m2:
                    gate_up(c1, m2 * 2 + 2, 0)
                    project_down(c1, m2 * 2 + 1, 1)
                    gate_up(c1, m2 * 2 + 3, 1)
                    project_down(c1, m2 * 2 + 2, 0)
                project_down(c1, MB - 1, 1, last=True)


def attention(nc, a, scr, out):
    with ExitStack() as ctx:
        def sb(name, shape, dt=F32):
            return ctx.enter_context(nc.sbuf_tensor(name, shape, dt))

        def bank(name, n=1):
            return ctx.enter_context(nc.psum_tensor(name, [P, n * 512], F32))

        def sem(name):
            return ctx.enter_context(nc.semaphore(name))

        ident = sb("ident2", [P, P])
        identb = sb("identb", [P, P], BF16)
        mask = sb("mask", [P, P], BF16)
        qtab = sb("qtab", [P, TB, 2, HALF])
        xT = sb("xT2", [P, 2, KC, S], F32R)
        acc = sb("acc", [P, TB, D])
        kT = sb("kT", [P, 2, 2, S], F32R)
        v_sb = sb("v_sb", [P, 2, 2, TB, DH], F32R)
        wq_raw = sb("wq_raw", [P, KC, GRP * DH])
        wq = sb("wq", [P, 2, KC, GRP * DH], F32R)
        wo_raw = sb("wo_raw", [P, GRP, D])
        wo = sb("wo", [P, 2, GRP, D], F32R)
        q_cos = sb("q_cos", [P, 512])
        q_sin = sb("q_sin", [P, 512])
        q_rot = sb("q_rot", [P, 512])
        qT = sb("qT", [P, 2, 2, 512], F32R)
        prob = sb("prob", [P, 2, GRP, S])
        pT = sb("pT", [P, 4, 2, 512], F32R)
        oT = sb("oT", [P, 2, 2, 512], F32R)
        nmax = sb("nmax", [P, 8])
        rsum = sb("rsum", [P, 8])
        rinv = sb("rinv", [P, 8])
        scores = [bank(f"scores{i}", 2) for i in range(2)]
        ptb = [bank(f"ptb{i}") for i in range(2)]
        ob = bank("ob")
        misc = bank("misc")

        const = sem("const")
        tab2 = sem("tab2")
        x_loaded = sem("x2_loaded")
        acc_loaded = sem("acc_loaded")
        acc_ready = sem("acc_ready")
        k_loaded = [sem(f"k_loaded{e}") for e in range(2)]
        v_loaded = [sem(f"v_loaded{e}") for e in range(2)]
        wq_loaded = sem("wq_loaded")
        wq_hi = sem("wq_hi")
        wq_split = sem("wq_split")
        wo_loaded = sem("wo_loaded")
        wo_hi = sem("wo_hi")
        wo_split = sem("wo_split")
        misc_done = sem("misc_done")
        misc_empty = sem("misc_empty")
        q_turned = sem("q_turned")
        qT_hi = sem("qT_hi")
        s_done = sem("s_done")
        max_ready = sem("max_ready")
        exp_done = sem("exp_done")
        inv_ready = sem("inv_ready")
        normed = sem("normed")
        t_done = sem("t_done")
        pT_hi = sem("pT_hi")
        pT_split = sem("pT_split")
        o_done = sem("o_done")
        oT_hi = sem("oT_hi")
        o_split = sem("o_split")
        stored = sem("out_stored")

        start_counts = [(misc_done, len(MISC)), (misc_empty, len(MISC)), (q_turned, UNITS),
                        (qT_hi, UNITS), (s_done, HPB), (max_ready, HPB), (exp_done, HPB),
                        (inv_ready, HPB), (normed, HPB), (t_done, KEYB), (pT_hi, KEYB),
                        (pT_split, KEYB), (o_done, UNITS), (oT_hi, UNITS), (o_split, UNITS),
                        (wq_loaded, 32), (wq_hi, 2), (wq_split, 2), (wo_loaded, 32), (wo_hi, 2),
                        (wo_split, 2), (k_loaded[0], 16), (k_loaded[1], 16), (v_loaded[0], 16),
                        (v_loaded[1], 16), (stored, 16)]
        with nc.Block() as start:
            @start.sync
            def _(sp):
                for s, n in start_counts:
                    sp.sem_inc(s, n)

        block = ctx.enter_context(nc.Block())

        def q_no(n):
            return MISC_NO[("Q", n, 0)]

        def w_no(n):
            return MISC_NO[("W", n, 0)]

        @block.sync
        def _(sp):
            sp.dma_start(qtab[:], a["qtab"]).then_inc(tab2, 16)
            with sp.Fori(0, B) as b:
                b1 = b * PAIRS + 1
                sp.wait_ge(misc_done, b1 * len(MISC))
                sp.dma_start(xT[:].bitcast(F32), scr["xT"][b]).then_inc(x_loaded, 16)
                sp.wait_ge(stored, b * 16 + 16)
                sp.dma_start(acc[:], scr["ffn"][b]).then_inc(acc_loaded, 16)
                sp.dma_start(prob[:, 1].rearrange("p a s -> p (a s)").rearrange("p (t d) -> p t d", d=D),
                             a["xp"][b]).then_inc(acc_loaded, 16)
                with sp.Fori(0, PAIRS) as pair:
                    it1 = b * PAIRS + pair + 1
                    for e in range(2):
                        sp.wait_ge(wq_split, it1 * 2 + e)
                        sp.dma_start(wq_raw[:], a["wq"][pair * 2 + e]).then_inc(wq_loaded, 16)
                        sp.wait_ge(s_done, it1 * HPB - (1 - e) * (HPB // 2))
                        sp.dma_start(kT[:, e].bitcast(F32), scr["k"][b, pair * 2 + e]).then_inc(k_loaded[e], 16)
                        sp.wait_ge(o_done, it1 * UNITS - (1 - e) * TB)
                        sp.dma_start(v_sb[:, e].bitcast(F32), scr["v"][b, pair * 2 + e]).then_inc(v_loaded[e], 16)
                        sp.wait_ge(wo_split, it1 * 2 + e)
                        sp.dma_start(wo_raw[:], a["wo"][pair * 2 + e]).then_inc(wo_loaded, 16)
                sp.wait_ge(misc_empty, (b + 1) * (PAIRS * len(MISC)) + len(MISC))
                sp.dma_start(out[b], acc[:]).then_inc(stored, 16)
            sp.wait_ge(stored, 16 * (B + 1))

        @block.gpsimd
        def _(pool):
            nc.gpsimd.memset(ident[:], 0.0).then_inc(const, 1)
            nc.gpsimd.memset(identb[:], 0.0).then_inc(const, 1)
            nc.gpsimd.memset(mask[:], 0.0).then_inc(const, 1)
            pool.wait_ge(const, 3)
            for m in (ident, identb):
                nc.gpsimd.affine_select(out=m[:], in_=m[:], compare_op=ALU.not_equal, fill=1.0,
                                        base=0, pattern=[[-1, P]], channel_multiplier=1).then_inc(const, 1)
            nc.gpsimd.affine_select(out=mask[:], in_=mask[:], compare_op=ALU.is_ge, fill=MASKED,
                                    base=0, pattern=[[-1, P]], channel_multiplier=1).then_inc(const, 1)
            with pool.Fori(0, B * PAIRS) as it:
                it1 = it + 1
                for kind, n, h in with_later("NORM", 3):
                    if kind == "NORM":
                        hd, W = n * GRP + h, key_blocks(n) * P
                        pool.wait_ge(inv_ready, it1 * HPB + hd + 1)
                        nc.gpsimd.tensor_tensor(prob[:, n % 2, h, 0:W], prob[:, n % 2, h, 0:W],
                                                rinv[:, hd % 8:hd % 8 + 1].broadcast_to([P, W]), ALU.mult)\
                            .then_inc(normed, 1)
                    elif kind == "Q":
                        qc, qs, qr = (v.rearrange("p (h f r) -> p h f r", f=2, r=HALF)
                                      for v in (q_cos[:], q_sin[:], q_rot[:]))
                        pool.wait_ge(misc_empty, it1 * len(MISC) + q_no(n) + 1)
                        if n == 0:
                            pool.wait_ge(misc_done, it1 * len(MISC))
                        else:
                            pool.wait_ge(misc_done, it1 * len(MISC) + MISC_NO[("QT", n - 1, 0)] + 1)
                        nc.gpsimd.tensor_tensor(qr[:, :, 0], qc[:, :, 0], qs[:, :, 0], ALU.subtract)
                        nc.gpsimd.tensor_tensor(qr[:, :, 1], qc[:, :, 1], qs[:, :, 1], ALU.add)\
                            .then_inc(q_turned, 1)

        @block.scalar
        def _(act):
            def split_q(it1, e):
                act.wait_ge(wq_loaded, (it1 * 2 + e + 1) * 16)
                if e:
                    act.wait_ge(misc_done, it1 * len(MISC) + q_no(TB - 1) + 1)
                else:
                    act.wait_ge(misc_done, it1 * len(MISC))
                nc.scalar.activation(wq[:, HI], wq_raw[:], ACT.Copy).then_inc(wq_hi, 1)

            def split_o(it1, e):
                act.wait_ge(wo_loaded, (it1 * 2 + e + 1) * 16)
                if e:
                    act.wait_ge(misc_done, it1 * len(MISC) + w_no(TB - 1) + 1)
                else:
                    act.wait_ge(misc_done, it1 * len(MISC))
                nc.scalar.activation(wo[:, HI], wo_raw[:], ACT.Copy).then_inc(wo_hi, 1)

            act.wait_ge(const, 6)
            with act.Fori(0, B * PAIRS) as it:
                it1 = it + 1
                split_q(it1, 0)
                for kind, n, j in with_later("EXP", 2):
                    if kind == "EXP":
                        hd, W = n * GRP + j, key_blocks(n) * P
                        act.wait_ge(max_ready, it1 * HPB + hd + 1)
                        act.wait_ge(inv_ready, it1 * HPB + hd - 7)
                        nc.scalar.activation(prob[:, n % 2, j, 0:W], scores[hd % 2][:, 0:W], ACT.Exp,
                                             bias=nmax[:, hd % 8:hd % 8 + 1],
                                             accum_out=rsum[:, hd % 8:hd % 8 + 1]).then_inc(exp_done, 1)
                    elif kind == "QT":
                        if n == 0:
                            split_o(it1, 0)
                        act.wait_ge(misc_done, it1 * len(MISC) + MISC_NO[("QT", n, 0)] + 1)
                        nc.scalar.activation(qT[:, n % 2, HI], misc[:], ACT.Copy).then_inc(qT_hi, 1)
                    elif kind == "T":
                        t = first_key_block(n) + j
                        act.wait_ge(t_done, it1 * KEYB + t + 1)
                        nc.scalar.activation(pT[:, t % 4, HI], ptb[t % 2][:], ACT.Copy).then_inc(pT_hi, 1)
                    elif kind == "PV" and j == key_blocks(n) - 1:
                        act.wait_ge(o_done, it1 * UNITS + n + 1)
                        nc.scalar.activation(oT[:, n % 2, HI], ob[:], ACT.Copy).then_inc(oT_hi, 1)
                    elif kind == "Q" and n == TB - 1:
                        split_q(it1, 1)
                    elif kind == "W" and n == TB - 1:
                        split_o(it1, 1)

        @block.vector
        def _(dve):
            def split_q(it1, e):
                dve.wait_ge(wq_hi, it1 * 2 + e + 1)
                nc.vector.tensor_tensor(wq[:, LO], wq_raw[:], wq[:, HI].bitcast(F32), ALU.subtract)\
                    .then_inc(wq_split, 1)

            def split_o(it1, e):
                dve.wait_ge(wo_hi, it1 * 2 + e + 1)
                nc.vector.tensor_tensor(wo[:, LO], wo_raw[:], wo[:, HI].bitcast(F32), ALU.subtract)\
                    .then_inc(wo_split, 1)

            dve.wait_ge(tab2, 16)
            with dve.Fori(0, B) as b:
                dve.wait_ge(acc_loaded, b * 32 + 32)
                nc.vector.tensor_tensor(acc[:].rearrange("p t d -> p (t d)"),
                                        acc[:].rearrange("p t d -> p (t d)"),
                                        prob[:, 1].rearrange("p a s -> p (a s)"), ALU.add)\
                    .then_inc(acc_ready, 1)
                with dve.Fori(0, PAIRS) as pair:
                    it1 = b * PAIRS + pair + 1
                    dve.wait_ge(acc_ready, b + 1)
                    split_q(it1, 0)
                    for kind, n, j in with_later("INV", 4):
                        if kind == "S":
                            hd, W = n * GRP + j, key_blocks(n) * P
                            dve.wait_ge(s_done, it1 * HPB + hd + 1)
                            dve.wait_ge(exp_done, it1 * HPB + hd - 7)
                            nc.vector.tensor_reduce(nmax[:, hd % 8:hd % 8 + 1], scores[hd % 2][:, 0:W],
                                                    AX.X, ALU.max, negate=True).then_inc(max_ready, 1)
                        elif kind == "Q":
                            q, qc, qs = (v.rearrange("p (h f r) -> p h f r", f=2, r=HALF)
                                         for v in (misc[:], q_cos[:], q_sin[:]))
                            cos, sin = (qtab[:, unit_block(n), x].unsqueeze(1).broadcast_to([P, GRP, HALF])
                                        for x in range(2))
                            dve.wait_ge(misc_done, it1 * len(MISC) + q_no(n) + 1)
                            dve.wait_ge(q_turned, it1 * UNITS + n)
                            for f in range(2):
                                nc.vector.tensor_tensor(qc[:, :, f], q[:, :, f], cos, ALU.mult)
                            nc.vector.tensor_tensor(qs[:, :, 0], q[:, :, 1], sin, ALU.mult)
                            nc.vector.tensor_tensor(qs[:, :, 1], q[:, :, 0], sin, ALU.mult)\
                                .then_inc(misc_empty, 1)
                            if n == TB - 1:
                                split_q(it1, 1)
                        elif kind == "QT":
                            if n == 0:
                                split_o(it1, 0)
                            dve.wait_ge(qT_hi, it1 * UNITS + n + 1)
                            nc.vector.tensor_tensor(qT[:, n % 2, LO], misc[:], qT[:, n % 2, HI].bitcast(F32),
                                                    ALU.subtract).then_inc(misc_empty, 1)
                        elif kind == "T":
                            t = first_key_block(n) + j
                            dve.wait_ge(pT_hi, it1 * KEYB + t + 1)
                            nc.vector.tensor_tensor(pT[:, t % 4, LO], ptb[t % 2][:], pT[:, t % 4, HI].bitcast(F32),
                                                    ALU.subtract).then_inc(pT_split, 1)
                        elif kind == "PV" and j == key_blocks(n) - 1:
                            dve.wait_ge(oT_hi, it1 * UNITS + n + 1)
                            nc.vector.tensor_tensor(oT[:, n % 2, LO], ob[:], oT[:, n % 2, HI].bitcast(F32),
                                                    ALU.subtract).then_inc(o_split, 1)
                        elif kind == "W":
                            i_b = unit_block(n)
                            dve.wait_ge(misc_done, it1 * len(MISC) + w_no(n) + 1)
                            nc.vector.tensor_tensor(acc[:, i_b], misc[:], acc[:, i_b], ALU.add)\
                                .then_inc(misc_empty, 1)
                            if n == TB - 1:
                                split_o(it1, 1)
                        elif kind == "INV":
                            hd = n * GRP + j
                            dve.wait_ge(exp_done, it1 * HPB + hd + 1)
                            dve.wait_ge(normed, it1 * HPB + hd - 7)
                            nc.vector.reciprocal(rinv[:, hd % 8:hd % 8 + 1], rsum[:, hd % 8:hd % 8 + 1])\
                                .then_inc(inv_ready, 1)

        @block.tensor
        def _(pe):
            pe.wait_ge(const, 6)
            with pe.Fori(0, B) as b:
                with pe.Fori(0, PAIRS) as pair:
                    it1 = b * PAIRS + pair + 1
                    pe.wait_ge(x_loaded, b * 16 + 16)
                    for kind, n, j in SCHEDULE:
                        e, i, u = unit_kv(n), unit_block(n), n % 2
                        if kind in ("Q", "QT", "W"):
                            pe.wait_ge(misc_empty, it1 * len(MISC) + MISC_NO[(kind, n, 0)])
                        if kind == "Q":
                            if n % TB == 0:
                                pe.wait_ge(wq_split, it1 * 2 + e + 1)
                            pairs = [(xT[:, x, k, i * P:(i + 1) * P], wq[:, w, k])
                                     for k in range(KC) for x, w in PASSES]
                            for m, (l, r) in enumerate(pairs):
                                mm = nc.tensor.matmul(misc[:], l, r, start=(m == 0), stop=(m == len(pairs) - 1))
                            mm.then_inc(misc_done, 1)
                        elif kind == "QT":
                            pe.wait_ge(q_turned, it1 * UNITS + n + 1)
                            for h in range(GRP):
                                mm = nc.tensor.transpose(misc[:, h * P:(h + 1) * P], q_rot[:, h * P:(h + 1) * P], ident[:])
                            mm.then_inc(misc_done, 1)
                        elif kind == "S":
                            hd, W = n * GRP + j, (i + 1) * P
                            if j == 0:
                                pe.wait_ge(misc_empty, it1 * len(MISC) + MISC_NO[("QT", n, 0)] + 1)
                                if n % TB == 0:
                                    pe.wait_ge(k_loaded[e], it1 * 16 + 16)
                            pe.wait_ge(exp_done, it1 * HPB + hd - 1)
                            sc = scores[hd % 2]
                            cuts = [(c, min(c + 512, W)) for c in range(0, W, 512)]
                            for x, y in PASSES:
                                for c0, c1 in cuts:
                                    mm = nc.tensor.matmul(sc[:, c0:c1], qT[:, u, x, j * P:(j + 1) * P],
                                                          kT[:, e, y, c0:c1], start=(x == HI and y == HI),
                                                          stop=(x == LO))
                                if (x, y) == (HI, HI):
                                    nc.tensor.matmul(sc[:, W - P:W], identb[:], mask[:], start=False, stop=False)
                            mm.then_inc(s_done, 1)
                        elif kind == "T":
                            t = first_key_block(n) + j
                            if j == 0:
                                pe.wait_ge(normed, it1 * HPB + (n + 1) * GRP)
                            pe.wait_ge(pT_split, it1 * KEYB + t - 1)
                            for h in range(GRP):
                                mm = nc.tensor.transpose(ptb[t % 2][:, h * P:(h + 1) * P],
                                                         prob[:, u, h, j * P:(j + 1) * P], ident[:])
                            mm.then_inc(t_done, 1)
                        elif kind == "PV":
                            t = first_key_block(n) + j
                            if j == 0:
                                pe.wait_ge(o_split, it1 * UNITS + n)
                                if n % TB == 0:
                                    pe.wait_ge(v_loaded[e], it1 * 16 + 16)
                            pe.wait_ge(pT_split, it1 * KEYB + t + 1)
                            for x, y in PASSES:
                                mm = nc.tensor.matmul(ob[:], v_sb[:, e, x, j], pT[:, t % 4, y],
                                                      start=(j == 0 and (x, y) == (HI, HI)),
                                                      stop=(j == i and x == LO))
                            if j == i:
                                mm.then_inc(o_done, 1)
                        elif kind == "W":
                            if n % TB == 0:
                                pe.wait_ge(wo_split, it1 * 2 + e + 1)
                            pe.wait_ge(o_split, it1 * UNITS + n + 1)
                            pairs = [(oT[:, u, x, h * P:(h + 1) * P], wo[:, w, h])
                                     for h in range(GRP) for x, w in PASSES]
                            for m, (l, r) in enumerate(pairs):
                                mm = nc.tensor.matmul(misc[:], l, r, start=(m == 0), stop=(m == len(pairs) - 1))
                            mm.then_inc(misc_done, 1)


def build(nc, a, out):
    scr = {
        "xT": nc.dram_tensor("xT_parts", [B, P, 2, KC, S], F32, kind="Internal").ap(),
        "k": nc.dram_tensor("k_parts", [B, KVH, P, 2, S], F32, kind="Internal").ap(),
        "v": nc.dram_tensor("v_parts", [B, KVH, P, 2, TB, DH], F32, kind="Internal").ap(),
        "ffn": nc.dram_tensor("ffn_out", [B, P, TB, D], F32, kind="Internal").ap(),
    }
    key_value_and_ffn(nc, a, scr, [])
    attention(nc, a, scr, out)


def kernel(L0_attn_hidden_states, L0_attn_Wq, L0_attn_Wkr, L0_attn_Wdk, L0_attn_Wupk, L0_attn_Wupv,
           L0_attn_Wo, L0_ffn_W_gate, L0_ffn_W_up, L0_ffn_W_down):
    import numpy as np
    import concourse.bacc as bacc
    from concourse.bass_utils import run_bass_kernel_spmd

    x, Wq, Wkr, Wdk, Wupk, Wupv, Wo, Wg, Wu, Wd = (np.asarray(v) for v in (
        L0_attn_hidden_states, L0_attn_Wq, L0_attn_Wkr, L0_attn_Wdk, L0_attn_Wupk, L0_attn_Wupv,
        L0_attn_Wo, L0_ffn_W_gate, L0_ffn_W_up, L0_ffn_W_down))

    def by_partition(wt, cols):
        k, n = wt.shape
        return wt.reshape(k // P, P, n // cols, cols).transpose(2, 1, 0, 3)

    gate, up = (by_partition(w.T, P).reshape(MB, P, C) for w in (Wg, Wu))
    inv_freq = 1.0 / 10000.0 ** (np.arange(0, DH, 2, dtype=np.float32) / DH)
    freqs = np.outer(np.arange(S, dtype=np.float32), inv_freq)
    cs = np.stack([np.cos(freqs), np.sin(freqs)], 1).astype(np.float32)
    scale = np.float32(1.0) / np.sqrt(np.float32(DH))
    arrays = {
        "x": x.reshape(B, S // CHUNK, CT, P, D).transpose(0, 1, 3, 2, 4),
        "xp": x.reshape(B, TB, P, D).transpose(0, 2, 1, 3),
        "wq": by_partition(Wq.T, GRP * DH),
        "wkr": by_partition(Wkr.T, 512)[0],
        "wdk": by_partition(Wdk.T, 512)[0],
        "wupk": by_partition(Wupk.T, 512)[0],
        "wupv": by_partition(Wupv.T, 512),
        "wo": Wo.T.reshape(KVH, GRP, DH, D).transpose(0, 2, 1, 3),
        "ffw": np.concatenate([gate, up, Wd.T.reshape(MB, P, D)], axis=2),
        "ktab": cs[:, :, 0:RH].reshape(S // CHUNK, CT, P, 2, RH).transpose(0, 2, 1, 3, 4),
        "qtab": (cs * scale).reshape(TB, P, 2, HALF).transpose(1, 0, 2, 3),
    }
    arrays = {k: np.ascontiguousarray(v) for k, v in arrays.items()}
    nc = bacc.Bacc("TRN2", target_bir_lowering=False, num_devices=1)
    a = {k: nc.dram_tensor(f"in_{k}", v.shape, mybir.dt.from_np(v.dtype), kind="ExternalInput").ap()
         for k, v in arrays.items()}
    out = nc.dram_tensor("out", [B, P, TB, D], F32, kind="ExternalOutput").ap()
    build(nc, a, out)
    r = run_bass_kernel_spmd(nc, [{f"in_{k}": v for k, v in arrays.items()}], core_ids=[0])
    return np.ascontiguousarray(r.results[0]["out"].transpose(0, 2, 1, 3)).reshape(B, S, D)
```

```python
from contextlib import ExitStack

import concourse.bass as bass
from concourse import mybir

F32 = mybir.dt.float32
F32R = mybir.dt.float32r
F16 = mybir.dt.float16
BF16 = mybir.dt.bfloat16
ACT = mybir.ActivationFunctionType
ALU = mybir.AluOpType
AX = mybir.AxisListType

HI, LO = 0, 1
PASSES = ((HI, HI), (HI, LO), (LO, HI))

P = 128
B, S, D = 2, 1024, 512
HEADS, KVH, DH = 32, 8, 128
GRP = HEADS // KVH
HALF = DH // 2
RH = 32
KC = D // P
C = 512
CC = C // P
M = 1792
MB = M // P
TB = S // P
CHUNK = 512
CT = CHUNK // P
CHUNKS = B * S // CHUNK
FFW = 3 * C
EPS = 1e-5
MASKED = -1e30

RING = 4
G_XT = 0
G_KR = G_XT + KC
G_CT = G_KR + CT
G_KRT = G_CT + CC
G_KN = G_KRT + KVH // 2
G_V = G_KN + KVH // 2
GROUPS = G_V + 2 * CT
STORED = range(G_KRT, GROUPS)
SPLITS = GROUPS - CT


def split_no(n):
    return n + 1 if n < G_KR else n + 1 - CT


def stores_upto(slot, n):
    return sum(4 if m < G_V else 2 for m in STORED if m % RING == slot and m <= n)


PAIRS = KVH // 2
BODIES = B * PAIRS
UNITS = 2 * TB
HPB = UNITS * GRP
EARLY = 2


def unit_kv(n):
    return n // TB


def unit_block(n):
    return n % TB if n // TB % 2 == 0 else TB - 1 - n % TB


def key_blocks(n):
    return unit_block(n) + 1


def first_key_block(n):
    return sum(key_blocks(m) for m in range(n))


KEYB = first_key_block(UNITS)


def schedule(units):
    out = [("XQ", 0, p) for p in range(KC)] + [("Q", 0, 0), ("QT", 0, 0), ("Q", 1, 0)]
    turned = []

    def transpose(n, j):
        out.append(("T", n, j))
        turned.append((n, j))
        if len(turned) > LAG:
            out.append(("PV", *turned.pop(0)))

    for k in range(units + 2):
        if k % UNITS == EARLY and k < units:
            out.append(("CUT", k - EARLY, 0))
        real, blocks = k < units, key_blocks(k - 1) if 1 <= k <= units else 0
        xq = [[("XQ", m, p) for p in range(KC)] if m % TB == 0 and 0 < m < units else []
              for m in (k + 3, k + 2)]
        xo = [("XO", k - 1, p) for p in range(GRP)] if (k - 1) % TB == 0 and k - 1 < units else []
        qt = [("QT", k + 1, 0)] if k + 1 < units else []

        def soft(name, h):
            return [(name, k, h)] if real else []

        out += soft("S", 0)
        if blocks > QT_SHORT:
            out += qt
        if blocks:
            transpose(k - 1, 0)
        while turned and turned[0][0] < k - 1:
            out.append(("PV", *turned.pop(0)))
        out += soft("EXP", 0) + xq[1][2:3] + soft("INV", 0)
        out += soft("S", 1) + soft("NORM", 0)
        if blocks > 1:
            transpose(k - 1, 1)
        if blocks <= QT_SHORT:
            out += qt
        out += soft("EXP", 1) + xq[1][3:4]
        out += soft("S", 2) + soft("INV", 1) + soft("NORM", 1) + soft("EXP", 2)
        out += soft("INV", 2) + soft("NORM", 2)
        if k >= 2:
            out.append(("W", k - 2, 0))
        out += soft("S", 3) + soft("EXP", 3) + soft("INV", 3) + soft("NORM", 3) + xo[0:2]
        if k + 2 < units:
            out.append(("Q", k + 2, 0))
        for j in range(2, max(blocks, 4)):
            if j < blocks:
                transpose(k - 1, j)
            out += xq[0][j - 2:j - 1] + xo[j:j + 1] if j < 4 else []
    return out


LAG = 2
QT_SHORT = 2
WHOLE = schedule(3 * UNITS)
MISC_NO = {e[:2]: i for i, e in enumerate(e for e in WHOLE if e[0] in ("Q", "QT", "W"))}
MPB = 3 * UNITS
Q_TO_W = 4


def cut(seq):
    c = [i for i, e in enumerate(seq) if e[0] == "CUT"]
    first, body, again, last = seq[:c[0]], seq[c[0] + 1:c[1]], seq[c[1] + 1:c[2]], seq[c[2] + 1:]
    assert [(k, n - UNITS, j) for k, n, j in again] == body
    return first, body, last


def key_value_and_ffn(nc, a, scr, prime):
    with ExitStack() as ctx:
        def sb(name, shape, dt=F32):
            return ctx.enter_context(nc.sbuf_tensor(name, shape, dt))

        def bank(name):
            return ctx.enter_context(nc.psum_tensor(name, [P, 512], F32))

        def sem(name):
            return ctx.enter_context(nc.semaphore(name))

        ident = sb("ident1", [P, P])
        w_raw = sb("w_raw", [P, 4, 512])
        w_raw2 = sb("w_raw2", [P, 4, 512])
        ff_out = w_raw
        wdk = sb("wdk", [P, 2, KC, C], F32R)
        wkr = sb("wkr", [P, 2, KC, 512], F32R)
        wupk = sb("wupk", [P, 2, CC, 512], F32R)
        wupv = sb("wupv", [P, 2, 2, CC, 512], F32R)
        ktab = sb("ktab", [P, CT, 2, RH])
        x_in = sb("x_in", [P, CT, D])
        xn = sb("xn", [P, CT, D])
        stats = sb("stats", [P, CT, 6])
        mv = sb("mv", [P, CT, 2])
        var_eps = sb("var_eps", [P, CT])
        power = sb("power", [P, CT])
        rstd = sb("rstd", [P, CT])
        xT = sb("xT1", [P, 2, KC, CHUNK], F32R)
        cT = sb("cT", [P, 2, CC, CHUNK], F32R)
        k_cos = sb("k_cos", [P, 512])
        k_sin = sb("k_sin", [P, 512])
        k_rot = sb("k_rot", [P, CT, 512])
        stage = sb("stage", [P, RING, 2, 512], F32R)
        ff_raw = sb("ff_raw", [P, 2, FFW], F16)
        ff_w = sb("ff_w", [P, 2, FFW], F32R)
        silu = sb("silu", [P, 512])
        h32 = sb("h32", [P, 512])
        hT = sb("hT", [P, 2, 2, 512], F32R)
        ring = [bank(f"ring{i}") for i in range(RING)]
        down = [bank(f"down{i}") for i in range(CT)]

        ident_ready = sem("ident_ready")
        w_loaded = [sem(f"w_loaded{i}") for i in range(5)]
        w_hi = sem("w_hi")
        w_split = sem("w_split")
        x_loaded = sem("x_loaded")
        tab_loaded = sem("tab_loaded")
        ln_step = sem("ln_step")
        rstd_ready = sem("rstd_ready")
        xn_ready = sem("xn_ready")
        group_done = sem("group_done")
        hi_ready = sem("hi_ready")
        emptied = sem("emptied")
        rotated = sem("rotated")
        stored = [sem(f"stored{i}") for i in range(RING)]
        xT_stored = sem("xT_stored")
        ff_loaded = [sem(f"ff_loaded{i}") for i in range(2)]
        gate_up_cast = sem("gate_up_cast")
        down_cast = sem("down_cast")
        gate_done = sem("gate_done")
        up_done = sem("up_done")
        res_loaded = sem("res_loaded")
        silu_ready = sem("silu_ready")
        h_ready = sem("h_ready")
        h_hi = sem("h_hi")
        h_split = sem("h_split")
        down_done = sem("down_done")
        ff_copied = sem("ff_copied")
        ff_stored = sem("ff_stored")

        prime += [(group_done, GROUPS), (hi_ready, SPLITS), (emptied, GROUPS), (rotated, CT),
                  (xn_ready, CT), (xT_stored, 16 * CT), (gate_up_cast, MB), (down_cast, MB), (gate_done, MB),
                  (up_done, MB), (silu_ready, MB), (h_ready, MB), (h_hi, MB), (h_split, MB),
                  (down_done, MB), (ff_copied, CT), (x_loaded, 16), (tab_loaded, 16),
                  (ff_loaded[0], 16 * MB // 2), (ff_loaded[1], 16 * MB // 2),
                  (ff_stored, 16),
                  (ln_step, 2), (rstd_ready, 1)]
        prime += [(stored[s], 16 * stores_upto(s, GROUPS)) for s in range(RING)]
        with nc.Block() as start:
            @start.sync
            def _(sp):
                for s, n in prime:
                    sp.sem_inc(s, n)

        weights = [(a["wkr"], wkr), (a["wdk"], wdk), (a["wupk"], wupk)]
        weights = [(src, dst[:, HI], dst[:, LO]) for src, dst in weights]
        weights += [(a["wupv"][v], wupv[:, HI, v], wupv[:, LO, v]) for v in range(2)]
        raw = [w_raw, k_rot, w_raw2, w_raw, w_raw2]
        split_ahead = {G_XT: (0,), G_KR: (1,), G_CT: (2,), G_KRT: (3, 4)}
        block = ctx.enter_context(nc.Block())

        @block.sync
        def _(sp):
            def load_x(c):
                sp.wait_ge(xn_ready, (c + 1) * CT)
                sp.dma_start(x_in[:], a["x"][c]).then_inc(x_loaded, 16)
                sp.wait_ge(emptied, c * GROUPS + G_CT)
                sp.dma_start(ktab[:], a["ktab"][c]).then_inc(tab_loaded, 16)

            def load_ff(c1, m, o):
                sp.wait_ge(down_cast, c1 * MB + m - 1)
                sp.dma_start(ff_raw[:, o], a["ffw"][m]).then_inc(ff_loaded[o], 16)

            def chunk(c, last=False):
                c1 = c + 1
                sp.wait_ge(emptied, c1 * GROUPS + G_KR)
                for t in range(CT):
                    sp.dma_start(scr["xT"][c * CT + t].rearrange("p a k s -> p (a k) s"),
                                 xT[:, :, :, t * P:(t + 1) * P].bitcast(F32)
                                 .rearrange("p a k s -> p (a k) s")).then_inc(xT_stored, 16)
                load_ff(c1, 0, 0)
                load_ff(c1, 1, 1)
                if not last:
                    load_x(c + 1)
                for n in STORED:
                    s = n % RING
                    sp.wait_ge(emptied, c1 * GROUPS + n + 1)
                    if n < G_V:
                        pair, low = (n - G_KRT, 0) if n < G_KN else (n - G_KN, RH)
                        for q in range(4):
                            row = (q % 2) * HALF + low
                            sp.dma_start(scr["k"][2 * pair + q // 2, row:row + RH, :,
                                                  bass.ds(c * CHUNK, CHUNK)],
                                         stage[q * RH:(q + 1) * RH, s].bitcast(F32))\
                                .then_inc(stored[s], 16)
                    else:
                        t, v = (n - G_V) // 2, (n - G_V) % 2
                        for part in (HI, LO):
                            sp.dma_start(
                                scr["v"][v * 4:v * 4 + 4, :, part, c * CT + t, :]
                                .rearrange("g p d -> p g d"),
                                stage[:, s, part].bitcast(F32).rearrange("p (g d) -> p g d", g=4))\
                                .then_inc(stored[s], 16)
                sp.wait_ge(w_split, len(weights))
                sp.wait_ge(ff_stored, c1 * 16)
                sp.dma_start(ff_out[:], a["x"][c]).then_inc(res_loaded, 16)
                with sp.Fori(1, MB // 2) as m2:
                    for o in range(2):
                        load_ff(c1, m2 * 2 + o, o)

            load_x(0)
            for n, (src, _, _) in enumerate(weights):
                if n > 2:
                    sp.wait_ge(w_split, (n - 3) * 2 + 1)
                sp.dma_start(raw[n][:], src).then_inc(w_loaded[n], 16)
            with sp.Fori(0, CHUNKS - 1) as c:
                chunk(c)
            chunk(CHUNKS - 1, last=True)
            sp.wait_ge(xT_stored, 16 * CT * (CHUNKS + 1))
            for s in range(RING):
                sp.wait_ge(stored[s], 16 * stores_upto(s, GROUPS) * (CHUNKS + 1))
            sp.wait_ge(ff_stored, 16 * (CHUNKS + 1))

        @block.gpsimd
        def _(pool):
            nc.gpsimd.memset(power[:], -0.5).then_inc(ident_ready, 1)
            nc.gpsimd.memset(ident[:], 0.0).then_inc(ident_ready, 1)
            pool.wait_ge(ident_ready, 2)
            nc.gpsimd.affine_select(out=ident[:], in_=ident[:], compare_op=ALU.not_equal, fill=1.0,
                                    base=0, pattern=[[-1, P]], channel_multiplier=1)\
                .then_inc(ident_ready, 1)

            def rstd_of(c1):
                pool.wait_ge(ln_step, c1 * 2 + 2)
                nc.gpsimd.tensor_tensor(rstd[:], var_eps[:], power[:], ALU.pow).then_inc(rstd_ready, 1)

            def rotate(c1):
                for t in range(CT):
                    kc, ks, kr = (v.rearrange("p (g h r) -> p g h r", h=2, r=RH)
                                  for v in (k_cos[:], k_sin[:], k_rot[:, t]))
                    pool.wait_ge(emptied, c1 * GROUPS + G_KR + t + 1)
                    nc.gpsimd.tensor_tensor(kr[:, :, 0], kc[:, :, 0], ks[:, :, 0], ALU.subtract)
                    nc.gpsimd.tensor_tensor(kr[:, :, 1], kc[:, :, 1], ks[:, :, 1], ALU.add)\
                        .then_inc(rotated, 1)

            rstd_of(1)
            pool.wait_ge(w_split, 2)
            with pool.Fori(0, CHUNKS - 1) as c:
                rotate(c + 1)
                rstd_of(c + 2)
            rotate(CHUNKS)

        @block.scalar
        def _(act):
            def split_weights(ns):
                for n in ns:
                    act.wait_ge(w_loaded[n], 16)
                    nc.scalar.activation(weights[n][1], raw[n][:], ACT.Copy).then_inc(w_hi, 1)

            def cast_gate_up(c1, m, o):
                act.wait_ge(ff_loaded[o], (c1 * MB + m + (2 - o)) * 8)
                act.wait_ge(up_done, c1 * MB + m - 1)
                nc.scalar.activation(ff_w[:, o, 0:2 * C], ff_raw[:, o, 0:2 * C], ACT.Copy)\
                    .then_inc(gate_up_cast, 1)

            def cast_down(c1, m, o):
                act.wait_ge(down_done, c1 * MB + m - 1)
                nc.scalar.activation(ff_w[:, o, 2 * C:], ff_raw[:, o, 2 * C:], ACT.Copy)\
                    .then_inc(down_cast, 1)

            def gate(c1, m, o):
                act.wait_ge(gate_done, c1 * MB + m + 1)
                act.wait_ge(h_ready, c1 * MB + m)
                nc.scalar.activation(silu[:], ring[o][:], ACT.Silu).then_inc(silu_ready, 1)
                act.wait_ge(h_ready, c1 * MB + m + 1)
                act.wait_ge(down_done, c1 * MB + m - 1)
                nc.scalar.activation(hT[:, o, HI], h32[:], ACT.Copy).then_inc(h_hi, 1)

            def chunk(c1, first=False):
                for n in range(G_XT, GROUPS):
                    if first:
                        split_weights(split_ahead.get(n, ()))
                    if n == G_KR and not first:
                        store_ff(c1 - 1)
                    if n == G_V:
                        cast_gate_up(c1, 0, 0)
                    if n == G_V + 2:
                        cast_gate_up(c1, 1, 1)
                    if n == G_V + 4:
                        cast_down(c1, 0, 0)
                    if G_KR <= n < G_CT:
                        continue
                    act.wait_ge(group_done, c1 * GROUPS + n + 1)
                    if n < G_KR:
                        if n == 0:
                            act.wait_ge(xT_stored, c1 * (16 * CT))
                        dst = xT[:, HI, n - G_XT]
                    elif n < G_KRT:
                        dst = cT[:, HI, n - G_CT]
                    else:
                        s = n % RING
                        act.wait_ge(stored[s], c1 * (16 * stores_upto(s, GROUPS)) + 16 * stores_upto(s, n - 1))
                        dst = stage[:, s, HI]
                    nc.scalar.activation(dst, ring[n % RING][:], ACT.Copy).then_inc(hi_ready, 1)
                with act.Fori(0, MB // 2 - 1) as m2:
                    for o in range(2):
                        gate(c1, m2 * 2 + o, o)
                        cast_gate_up(c1, m2 * 2 + (o + 2), o)
                        cast_down(c1, m2 * 2 + (o + 1), 1 - o)
                gate(c1, MB - 2, 0)
                cast_down(c1, MB - 1, 1)
                gate(c1, MB - 1, 1)

            def store_ff(c1):
                act.wait_ge(ff_copied, c1 * CT + CT)
                act.dma_start(scr["ffn"][bass.ds(c1 * CT - CT, CT)].rearrange("t p d -> p t d"), ff_out[:])\
                    .then_inc(ff_stored, 16)

            chunk(1, first=True)
            with act.Fori(1, CHUNKS) as c:
                chunk(c + 1)
            store_ff(CHUNKS)

        @block.vector
        def _(dve):
            def split_weights(ns):
                for n in ns:
                    _, hi, lo = weights[n]
                    dve.wait_ge(w_hi, n + 1)
                    nc.vector.tensor_tensor(lo, raw[n][:], hi.bitcast(F32), ALU.subtract).then_inc(w_split, 1)

            def split_lo(c1, n, hi, lo):
                dve.wait_ge(hi_ready, c1 * SPLITS + split_no(n))
                nc.vector.tensor_tensor(lo, ring[n % RING][:], hi.bitcast(F32), ALU.subtract)\
                    .then_inc(emptied, 1)

            def hidden(c1, m, o):
                dve.wait_ge(up_done, c1 * MB + m + 1)
                dve.wait_ge(silu_ready, c1 * MB + m + 1)
                dve.wait_ge(h_split, c1 * MB + m)
                nc.vector.tensor_tensor(h32[:], ring[2 + o][:], silu[:], ALU.mult).then_inc(h_ready, 1)
                dve.wait_ge(h_hi, c1 * MB + m + 1)
                nc.vector.tensor_tensor(hT[:, o, LO], h32[:], hT[:, o, HI].bitcast(F32), ALU.subtract)\
                    .then_inc(h_split, 1)

            def layer_norm(c1):
                dve.wait_ge(x_loaded, c1 * 16 + 16)
                for t in range(CT):
                    nc.vector.bn_stats(stats[:, t], x_in[:, t])
                dve.drain()
                for t in range(CT):
                    ins = nc.vector.bn_aggr(mv[:, t], stats[:, t])
                ins.then_inc(ln_step, 1)
                dve.wait_ge(ln_step, c1 * 2 + 1)
                nc.vector.tensor_scalar(var_eps[:], mv[:, :, 1], EPS, None, ALU.add).then_inc(ln_step, 1)
                dve.wait_ge(rstd_ready, c1 + 1)
                dve.wait_ge(group_done, c1 * GROUPS - GROUPS + G_KR)
                for t in range(CT):
                    nc.vector.tensor_scalar(xn[:, t], x_in[:, t], mv[:, t, 0:1], rstd[:, t:t + 1],
                                            ALU.subtract, ALU.mult).then_inc(xn_ready, 1)

            def projections(c1, first=False):
                for n in range(G_XT, GROUPS):
                    if first:
                        split_weights(split_ahead.get(n, ()))
                    elif n == G_KR:
                        finish_ffn(c1 - 1)
                    if n < G_KR:
                        split_lo(c1, n, xT[:, HI, n - G_XT], xT[:, LO, n - G_XT])
                    elif n < G_CT:
                        turn_keys(c1, n)
                    else:
                        dst = cT[:, :, n - G_CT] if n < G_KRT else stage[:, n % RING]
                        split_lo(c1, n, dst[:, HI], dst[:, LO])

            def turn_keys(c1, n):
                t = n - G_KR
                k, kc, ks = (v.rearrange("p (g h r) -> p g h r", h=2, r=RH)
                             for v in (ring[n % RING][:], k_cos[:], k_sin[:]))
                cos, sin = (ktab[:, t, i].unsqueeze(1).broadcast_to([P, KVH, RH]) for i in range(2))
                if t == 0:
                    dve.wait_ge(tab_loaded, c1 * 16 + 16)
                dve.wait_ge(group_done, c1 * GROUPS + n + 1)
                dve.wait_ge(rotated, c1 * CT + t)
                for h in range(2):
                    nc.vector.tensor_tensor(kc[:, :, h], k[:, :, h], cos, ALU.mult)
                nc.vector.tensor_tensor(ks[:, :, 0], k[:, :, 1], sin, ALU.mult)
                nc.vector.tensor_tensor(ks[:, :, 1], k[:, :, 0], sin, ALU.mult).then_inc(emptied, 1)

            def ffn(c1):
                with dve.Fori(0, MB // 2) as m2:
                    for o in range(2):
                        hidden(c1, m2 * 2 + o, o)

            def finish_ffn(c1):
                dve.wait_ge(down_done, c1 * MB + MB)
                dve.wait_ge(res_loaded, c1 * 16)
                for t in range(CT):
                    nc.vector.tensor_tensor(ff_out[:, t], down[t][:], ff_out[:, t], ALU.add)\
                        .then_inc(ff_copied, 1)

            layer_norm(1)
            projections(1, first=True)
            layer_norm(2)
            ffn(1)
            with dve.Fori(1, CHUNKS - 1) as c:
                projections(c + 1)
                layer_norm(c + 2)
                ffn(c + 1)
            projections(CHUNKS)
            ffn(CHUNKS)
            finish_ffn(CHUNKS)

        @block.tensor
        def _(pe):
            def products(n, c1, pairs, out=None):
                pe.wait_ge(emptied, c1 * GROUPS + n + 1 - RING)
                for i, (l, r) in enumerate(pairs):
                    mm = nc.tensor.matmul(ring[n % RING][:], l, r, start=(i == 0), stop=(i == len(pairs) - 1))
                mm.then_inc(group_done, 1)

            def transposes(n, c1, blocks):
                pe.wait_ge(emptied, c1 * GROUPS + n + 1 - RING)
                for i, src in enumerate(blocks):
                    mm = nc.tensor.transpose(ring[n % RING][:, i * P:(i + 1) * P], src, ident[:])
                mm.then_inc(group_done, 1)

            def gate_up(c1, m, o):
                pe.wait_ge(gate_up_cast, c1 * MB + m + 1)
                pe.wait_ge(h_ready, c1 * MB + m - 1)
                for side, done in ((0, gate_done), (1, up_done)):
                    w = ff_w[:, o, side * C:(side + 1) * C]
                    for i in range(2 * KC):
                        mm = nc.tensor.matmul(ring[2 * side + o][:], w[:, (i // 2) * P:(i // 2 + 1) * P],
                                              xT[:, i % 2, i // 2], start=(i == 0), stop=(i == 2 * KC - 1))
                    mm.then_inc(done, 1)

            def project_down(c1, m, o, first=False, last=False):
                pe.wait_ge(down_cast, c1 * MB + m + 1)
                pe.wait_ge(h_split, c1 * MB + m + 1)
                for t in range(CT):
                    for part in (HI, LO):
                        mm = nc.tensor.matmul(down[t][:], hT[:, o, part, t * P:(t + 1) * P],
                                              ff_w[:, o, 2 * C:3 * C],
                                              start=(first and part == HI), stop=(last and part == LO))
                mm.then_inc(down_done, 1)

            pe.wait_ge(ident_ready, 3)
            with pe.Fori(0, CHUNKS) as c:
                c1 = c + 1
                pe.wait_ge(xn_ready, c1 * CT + CT)
                pe.wait_ge(h_ready, c1 * MB)
                for k in range(KC):
                    transposes(G_XT + k, c1, [xn[:, t, k * P:(k + 1) * P] for t in range(CT)])
                pe.wait_ge(emptied, c1 * GROUPS + G_KR)
                pe.wait_ge(w_split, 1)
                for t in range(CT):
                    products(G_KR + t, c1, [(xT[:, x, k, t * P:(t + 1) * P], wkr[:, w, k])
                                            for k in range(KC) for x, w in PASSES])
                pe.wait_ge(w_split, 2)
                for m in range(CC):
                    products(G_CT + m, c1, [(wdk[:, w, k, m * P:(m + 1) * P], xT[:, x, k])
                                            for k in range(KC) for w, x in PASSES])
                pe.wait_ge(rotated, c1 * CT + CT)
                for q in range(KVH // 2):
                    transposes(G_KRT + q, c1, [k_rot[:, t, q * P:(q + 1) * P] for t in range(CT)])
                pe.wait_ge(emptied, c1 * GROUPS + G_KRT)
                pe.wait_ge(w_split, len(weights))
                for q in range(KVH // 2):
                    products(G_KN + q, c1, [(wupk[:, w, k, q * P:(q + 1) * P], cT[:, x, k])
                                            for k in range(CC) for w, x in PASSES])
                for t in range(CT):
                    for v in range(2):
                        products(G_V + 2 * t + v, c1, [(cT[:, x, k, t * P:(t + 1) * P], wupv[:, w, v, k])
                                                       for k in range(CC) for x, w in PASSES])
                pe.wait_ge(emptied, c1 * GROUPS + GROUPS)
                gate_up(c1, 0, 0)
                gate_up(c1, 1, 1)
                pe.wait_ge(ff_copied, c1 * CT)
                project_down(c1, 0, 0, first=True)
                with pe.Fori(0, MB // 2 - 1) as m2:
                    gate_up(c1, m2 * 2 + 2, 0)
                    project_down(c1, m2 * 2 + 1, 1)
                    gate_up(c1, m2 * 2 + 3, 1)
                    project_down(c1, m2 * 2 + 2, 0)
                project_down(c1, MB - 1, 1, last=True)


def attention(nc, a, scr, out):
    with ExitStack() as ctx:
        def sb(name, shape, dt=F32):
            return ctx.enter_context(nc.sbuf_tensor(name, shape, dt))

        def bank(name, n=1):
            return ctx.enter_context(nc.psum_tensor(name, [P, n * 512], F32))

        def sem(name):
            return ctx.enter_context(nc.semaphore(name))

        ident = sb("ident2", [P, P])
        identb = sb("identb", [P, P], BF16)
        mask = sb("mask", [P, P], BF16)
        qtab = sb("qtab", [P, TB, 2, HALF])
        xT = sb("xT2", [P, TB, 2, KC, P], F32R)
        acc = sb("acc", [P, TB, D])
        kT = sb("kT", [P, 2, 2, S], F32R)
        v_sb = sb("v_sb", [P, 2, 2, TB, DH], F32R)
        wq_raw = sb("wq_raw", [P, KC, GRP * DH])
        wq = sb("wq", [P, 2, KC, GRP * DH], F32R)
        wo_raw = sb("wo_raw", [P, GRP, D])
        wo = sb("wo", [P, 2, GRP, D], F32R)
        q_cos = sb("q_cos", [P, 512])
        q_sin = sb("q_sin", [P, 512])
        q_rot = sb("q_rot", [P, 512])
        qT = sb("qT", [P, 2, 2, 512], F32R)
        prob = sb("prob", [P, 2, GRP, S])
        pT = sb("pT", [P, 4, 2, 512], F32R)
        oT = sb("oT", [P, 2, 2, 512], F32R)
        nmax = sb("nmax", [P, 8])
        rsum = sb("rsum", [P, 8])
        rinv = sb("rinv", [P, 8])
        scores = [bank(f"scores{i}", 2) for i in range(2)]
        ptb = [bank(f"ptb{i}") for i in range(2)]
        ob = bank("ob")
        misc = bank("misc")

        const = sem("const")
        tab2 = sem("tab2")
        x_ready = [sem(f"x_ready{i}") for i in range(TB)]
        acc_ready = [sem(f"acc_ready{i}") for i in range(TB)]
        k_loaded = [sem(f"k_loaded{e}") for e in range(2)]
        v_loaded = [sem(f"v_loaded{e}") for e in range(2)]
        wq_loaded = sem("wq_loaded")
        wq_hi = sem("wq_hi")
        wq_split = sem("wq_split")
        wo_loaded = sem("wo_loaded")
        wo_hi = sem("wo_hi")
        wo_split = sem("wo_split")
        misc_done = sem("misc_done")
        misc_empty = sem("misc_empty")
        q_turned = sem("q_turned")
        qT_hi = sem("qT_hi")
        s_done = sem("s_done")
        max_ready = sem("max_ready")
        exp_done = sem("exp_done")
        inv_ready = sem("inv_ready")
        normed = sem("normed")
        t_done = sem("t_done")
        pT_hi = sem("pT_hi")
        pT_split = sem("pT_split")
        o_done = sem("o_done")
        oT_hi = sem("oT_hi")
        o_split = sem("o_split")
        stored = sem("out_stored")

        start_counts = [(misc_done, MPB), (misc_empty, MPB), (q_turned, UNITS),
                        (qT_hi, UNITS), (s_done, HPB), (max_ready, HPB), (exp_done, HPB),
                        (inv_ready, HPB), (normed, HPB), (t_done, KEYB), (pT_hi, KEYB),
                        (pT_split, KEYB), (o_done, UNITS), (oT_hi, UNITS), (o_split, UNITS),
                        (wq_loaded, 32), (wq_hi, 2 * KC), (wq_split, 2 * KC), (wo_loaded, 32),
                        (wo_hi, 2 * GRP), (wo_split, 2 * GRP), (k_loaded[0], 16),
                        (k_loaded[1], 16), (v_loaded[0], 16), (v_loaded[1], 16)]
        with nc.Block() as start:
            @start.sync
            def _(sp):
                for s, n in start_counts:
                    sp.sem_inc(s, n)

        block = ctx.enter_context(nc.Block())

        def misc_no(kind, n):
            return MISC_NO[(kind, n)]

        @block.sync
        def _(sp):
            def head_loads(b, pair, e, first=False):
                it1 = b * PAIRS + pair + 1
                sp.wait_ge(wq_split, it1 * (2 * KC) + e * KC)
                sp.dma_start(wq_raw[:], a["wq"][pair * 2 + e]).then_inc(wq_loaded, 16)
                if first:
                    load_x(b, 0)
                    load_x(b, 1)
                sp.wait_ge(s_done, it1 * HPB - (1 - e) * (HPB // 2))
                sp.dma_start(kT[:, e].bitcast(F32), scr["k"][pair * 2 + e, :, :, bass.ds(b * S, S)]).then_inc(k_loaded[e], 16)
                sp.wait_ge(o_done, it1 * UNITS - (1 - e) * TB)
                sp.dma_start(v_sb[:, e].bitcast(F32), scr["v"][pair * 2 + e, :, :, bass.ds(b * TB, TB)]).then_inc(v_loaded[e], 16)
                sp.wait_ge(wo_split, it1 * (2 * GRP) + e * GRP)
                sp.dma_start(wo_raw[:], a["wo"][pair * 2 + e]).then_inc(wo_loaded, 16)

            def load_x(b, i):
                sp.dma_start(xT[:, i].bitcast(F32), scr["xT"][b * TB + i]).then_inc(x_ready[i], 16)

            def load_acc(b, i):
                sp.dma_start(acc[:, i], scr["ffn"][b * TB + i]).then_inc(acc_ready[i], 16)

            def store_out(b, i, it1, n):
                sp.wait_ge(misc_empty, it1 * MPB + misc_no("W", n - 1 - i) + 1)
                sp.dma_start(out[b, :, i], acc[:, i]).then_inc(stored, 16)

            def later_pairs(b):
                with sp.Fori(1, PAIRS) as pair:
                    head_loads(b, pair, 0)
                    for ready in (x_ready, acc_ready):
                        for i in range(TB):
                            sp.wait_ge(ready[i], (b * PAIRS + pair) * 16)
                            sp.sem_inc(ready[i], 16)
                    head_loads(b, pair, 1)

            sp.dma_start(qtab[:], a["qtab"]).then_inc(tab2, 16)
            head_loads(0, 0, 0, first=True)
            for i in range(2, TB):
                load_x(0, i)
            for i in range(TB):
                load_acc(0, i)
            head_loads(0, 0, 1)
            later_pairs(0)
            with sp.Fori(1, B) as b:
                head_loads(b, 0, 0)
                for k in range(TB + Q_TO_W):
                    if k < TB:
                        i = TB - 1 - k
                        sp.wait_ge(misc_done, b * (PAIRS * MPB) + misc_no("Q", UNITS - 1 - i) + 1)
                        load_x(b, i)
                    if k >= Q_TO_W:
                        i = TB + Q_TO_W - 1 - k
                        store_out(b - 1, i, b * PAIRS, UNITS)
                        sp.wait_ge(stored, b * (16 * TB) - 16 * i)
                        load_acc(b, i)
                head_loads(b, 0, 1)
                later_pairs(b)
            for i in reversed(range(TB)):
                store_out(B - 1, i, BODIES - 2, 3 * UNITS)
            sp.wait_ge(stored, 16 * B * TB)

        @block.gpsimd
        def _(pool):
            nc.gpsimd.memset(ident[:], 0.0).then_inc(const, 1)
            nc.gpsimd.memset(identb[:], 0.0).then_inc(const, 1)
            nc.gpsimd.memset(mask[:], 0.0).then_inc(const, 1)
            pool.wait_ge(const, 3)
            for m in (ident, identb):
                nc.gpsimd.affine_select(out=m[:], in_=m[:], compare_op=ALU.not_equal, fill=1.0,
                                        base=0, pattern=[[-1, P]], channel_multiplier=1).then_inc(const, 1)
            nc.gpsimd.affine_select(out=mask[:], in_=mask[:], compare_op=ALU.is_ge, fill=MASKED,
                                    base=0, pattern=[[-1, P]], channel_multiplier=1).then_inc(const, 1)

            def work(events, it1):
                for kind, n, h in events:
                    if kind == "NORM":
                        hd, W = n * GRP + h, key_blocks(n) * P
                        pool.wait_ge(inv_ready, it1 * HPB + hd + 1)
                        nc.gpsimd.tensor_tensor(prob[:, n % 2, h, 0:W], prob[:, n % 2, h, 0:W],
                                                rinv[:, hd % 8:hd % 8 + 1].broadcast_to([P, W]), ALU.mult)\
                            .then_inc(normed, 1)
                    elif kind == "Q":
                        qc, qs, qr = (v.rearrange("p (h f r) -> p h f r", f=2, r=HALF)
                                      for v in (q_cos[:], q_sin[:], q_rot[:]))
                        pool.wait_ge(misc_empty, it1 * MPB + misc_no("Q", n) + 1)
                        if n:
                            pool.wait_ge(misc_done, it1 * MPB + misc_no("QT", n - 1) + 1)
                        nc.gpsimd.tensor_tensor(qr[:, :, 0], qc[:, :, 0], qs[:, :, 0], ALU.subtract)
                        nc.gpsimd.tensor_tensor(qr[:, :, 1], qc[:, :, 1], qs[:, :, 1], ALU.add)\
                            .then_inc(q_turned, 1)

            first, body, last = cut(WHOLE)
            work(first, 1)
            with pool.Fori(0, BODIES - 1) as it:
                work(body, it + 1)
            work(last, BODIES - 2)

        @block.scalar
        def _(act):
            def work(events, it1):
                for kind, n, j in events:
                    if kind == "EXP":
                        hd, W = n * GRP + j, key_blocks(n) * P
                        act.wait_ge(max_ready, it1 * HPB + hd + 1)
                        act.wait_ge(inv_ready, it1 * HPB + hd - 7)
                        nc.scalar.activation(prob[:, n % 2, j, 0:W], scores[hd % 2][:, 0:W], ACT.Exp,
                                             bias=nmax[:, hd % 8:hd % 8 + 1],
                                             accum_out=rsum[:, hd % 8:hd % 8 + 1]).then_inc(exp_done, 1)
                    elif kind == "QT":
                        act.wait_ge(misc_done, it1 * MPB + misc_no("QT", n) + 1)
                        nc.scalar.activation(qT[:, n % 2, HI], misc[:], ACT.Copy).then_inc(qT_hi, 1)
                    elif kind == "T":
                        t = first_key_block(n) + j
                        act.wait_ge(t_done, it1 * KEYB + t + 1)
                        nc.scalar.activation(pT[:, t % 4, HI], ptb[t % 2][:], ACT.Copy).then_inc(pT_hi, 1)
                    elif kind == "PV" and j == key_blocks(n) - 1:
                        act.wait_ge(o_done, it1 * UNITS + n + 1)
                        nc.scalar.activation(oT[:, n % 2, HI], ob[:], ACT.Copy).then_inc(oT_hi, 1)
                    elif kind == "XQ":
                        if j == 0:
                            if n:
                                act.wait_ge(misc_done, it1 * MPB + misc_no("Q", n - 1) + 1)
                            act.wait_ge(wq_loaded, (it1 * 2 + unit_kv(n) + 1) * 16)
                        nc.scalar.activation(wq[:, HI, j], wq_raw[:, j], ACT.Copy).then_inc(wq_hi, 1)
                    elif kind == "XO":
                        if j == 0:
                            if n:
                                act.wait_ge(misc_done, it1 * MPB + misc_no("W", n - 1) + 1)
                            act.wait_ge(wo_loaded, (it1 * 2 + unit_kv(n) + 1) * 16)
                        nc.scalar.activation(wo[:, HI, j], wo_raw[:, j], ACT.Copy).then_inc(wo_hi, 1)

            first, body, last = cut(WHOLE)
            act.wait_ge(const, 6)
            work(first, 1)
            with act.Fori(0, BODIES - 1) as it:
                work(body, it + 1)
            work(last, BODIES - 2)

        @block.vector
        def _(dve):
            def work(events, it1):
                for kind, n, j in events:
                    if kind == "S":
                        hd, W = n * GRP + j, key_blocks(n) * P
                        dve.wait_ge(s_done, it1 * HPB + hd + 1)
                        dve.wait_ge(exp_done, it1 * HPB + hd - 7)
                        nc.vector.tensor_reduce(nmax[:, hd % 8:hd % 8 + 1], scores[hd % 2][:, 0:W],
                                                AX.X, ALU.max, negate=True).then_inc(max_ready, 1)
                    elif kind == "Q":
                        q, qc, qs = (v.rearrange("p (h f r) -> p h f r", f=2, r=HALF)
                                     for v in (misc[:], q_cos[:], q_sin[:]))
                        cos, sin = (qtab[:, unit_block(n), x].unsqueeze(1).broadcast_to([P, GRP, HALF])
                                    for x in range(2))
                        dve.wait_ge(misc_done, it1 * MPB + misc_no("Q", n) + 1)
                        dve.wait_ge(q_turned, it1 * UNITS + n)
                        for f in range(2):
                            nc.vector.tensor_tensor(qc[:, :, f], q[:, :, f], cos, ALU.mult)
                        nc.vector.tensor_tensor(qs[:, :, 0], q[:, :, 1], sin, ALU.mult)
                        nc.vector.tensor_tensor(qs[:, :, 1], q[:, :, 0], sin, ALU.mult)\
                            .then_inc(misc_empty, 1)
                    elif kind == "QT":
                        dve.wait_ge(qT_hi, it1 * UNITS + n + 1)
                        nc.vector.tensor_tensor(qT[:, n % 2, LO], misc[:], qT[:, n % 2, HI].bitcast(F32),
                                                ALU.subtract).then_inc(misc_empty, 1)
                    elif kind == "T":
                        t = first_key_block(n) + j
                        dve.wait_ge(pT_hi, it1 * KEYB + t + 1)
                        nc.vector.tensor_tensor(pT[:, t % 4, LO], ptb[t % 2][:], pT[:, t % 4, HI].bitcast(F32),
                                                ALU.subtract).then_inc(pT_split, 1)
                    elif kind == "PV" and j == key_blocks(n) - 1:
                        dve.wait_ge(oT_hi, it1 * UNITS + n + 1)
                        nc.vector.tensor_tensor(oT[:, n % 2, LO], ob[:], oT[:, n % 2, HI].bitcast(F32),
                                                ALU.subtract).then_inc(o_split, 1)
                    elif kind == "W":
                        i_b = unit_block(n)
                        if n % UNITS < TB:
                            dve.wait_ge(acc_ready[i_b], (it1 + n // UNITS) * 16)
                        dve.wait_ge(misc_done, it1 * MPB + misc_no("W", n) + 1)
                        nc.vector.tensor_tensor(acc[:, i_b], misc[:], acc[:, i_b], ALU.add)\
                            .then_inc(misc_empty, 1)
                    elif kind == "INV":
                        hd = n * GRP + j
                        dve.wait_ge(exp_done, it1 * HPB + hd + 1)
                        dve.wait_ge(normed, it1 * HPB + hd - 7)
                        nc.vector.reciprocal(rinv[:, hd % 8:hd % 8 + 1], rsum[:, hd % 8:hd % 8 + 1])\
                            .then_inc(inv_ready, 1)
                    elif kind == "XQ":
                        dve.wait_ge(wq_hi, (it1 * 2 + unit_kv(n)) * KC + j + 1)
                        nc.vector.tensor_tensor(wq[:, LO, j], wq_raw[:, j], wq[:, HI, j].bitcast(F32),
                                                ALU.subtract).then_inc(wq_split, 1)
                    elif kind == "XO":
                        dve.wait_ge(wo_hi, (it1 * 2 + unit_kv(n)) * GRP + j + 1)
                        nc.vector.tensor_tensor(wo[:, LO, j], wo_raw[:, j], wo[:, HI, j].bitcast(F32),
                                                ALU.subtract).then_inc(wo_split, 1)

            first, body, last = cut(WHOLE)
            dve.wait_ge(tab2, 16)
            work(first, 1)
            with dve.Fori(0, BODIES - 1) as it:
                work(body, it + 1)
            work(last, BODIES - 2)

        @block.tensor
        def _(pe):
            def work(events, it1):
                for kind, n, j in events:
                    e, i, u = unit_kv(n), unit_block(n), n % 2
                    if kind in ("Q", "QT", "W"):
                        pe.wait_ge(misc_empty, it1 * MPB + misc_no(kind, n))
                    if kind == "Q":
                        if n % UNITS < TB:
                            pe.wait_ge(x_ready[i], (it1 + n // UNITS) * 16)
                        for k in range(KC):
                            if n % TB == 0:
                                pe.wait_ge(wq_split, (it1 * 2 + e) * KC + k + 1)
                            for m, (x, w) in enumerate(PASSES):
                                mm = nc.tensor.matmul(misc[:], xT[:, i, x, k], wq[:, w, k],
                                                      start=(k == 0 and m == 0),
                                                      stop=(k == KC - 1 and m == len(PASSES) - 1))
                        mm.then_inc(misc_done, 1)
                    elif kind == "QT":
                        pe.wait_ge(q_turned, it1 * UNITS + n + 1)
                        for h in range(GRP):
                            mm = nc.tensor.transpose(misc[:, h * P:(h + 1) * P], q_rot[:, h * P:(h + 1) * P], ident[:])
                        mm.then_inc(misc_done, 1)
                    elif kind == "S":
                        hd, W = n * GRP + j, (i + 1) * P
                        if j == 0:
                            pe.wait_ge(misc_empty, it1 * MPB + misc_no("QT", n) + 1)
                            if n % TB == 0:
                                pe.wait_ge(k_loaded[e % 2], (it1 + n // UNITS) * 16 + 16)
                        pe.wait_ge(exp_done, it1 * HPB + hd - 1)
                        sc = scores[hd % 2]
                        cuts = [(c, min(c + 512, W)) for c in range(0, W, 512)]
                        for x, y in PASSES:
                            for c0, c1 in cuts:
                                mm = nc.tensor.matmul(sc[:, c0:c1], qT[:, u, x, j * P:(j + 1) * P],
                                                      kT[:, e % 2, y, c0:c1], start=(x == HI and y == HI),
                                                      stop=(x == LO))
                            if (x, y) == (HI, HI):
                                nc.tensor.matmul(sc[:, W - P:W], identb[:], mask[:], start=False, stop=False)
                        mm.then_inc(s_done, 1)
                    elif kind == "T":
                        t = first_key_block(n) + j
                        if j == 0:
                            pe.wait_ge(normed, it1 * HPB + (n + 1) * GRP)
                        pe.wait_ge(pT_split, it1 * KEYB + t - 1)
                        for h in range(GRP):
                            mm = nc.tensor.transpose(ptb[t % 2][:, h * P:(h + 1) * P],
                                                     prob[:, u, h, j * P:(j + 1) * P], ident[:])
                        mm.then_inc(t_done, 1)
                    elif kind == "PV":
                        t = first_key_block(n) + j
                        if j == 0:
                            pe.wait_ge(o_split, it1 * UNITS + n)
                            if n % TB == 0:
                                pe.wait_ge(v_loaded[e % 2], (it1 + n // UNITS) * 16 + 16)
                        pe.wait_ge(pT_split, it1 * KEYB + t + 1)
                        for x, y in PASSES:
                            mm = nc.tensor.matmul(ob[:], v_sb[:, e % 2, x, j], pT[:, t % 4, y],
                                                  start=(j == 0 and (x, y) == (HI, HI)),
                                                  stop=(j == i and x == LO))
                        if j == i:
                            mm.then_inc(o_done, 1)
                    elif kind == "W":
                        pe.wait_ge(o_split, it1 * UNITS + n + 1)
                        for h in range(GRP):
                            if n % TB == 0:
                                pe.wait_ge(wo_split, (it1 * 2 + e) * GRP + h + 1)
                            for m, (x, w) in enumerate(PASSES):
                                mm = nc.tensor.matmul(misc[:], oT[:, u, x, h * P:(h + 1) * P], wo[:, w, h],
                                                      start=(h == 0 and m == 0),
                                                      stop=(h == GRP - 1 and m == len(PASSES) - 1))
                        mm.then_inc(misc_done, 1)

            first, body, last = cut(WHOLE)
            pe.wait_ge(const, 6)
            work(first, 1)
            with pe.Fori(0, BODIES - 1) as it:
                work(body, it + 1)
            work(last, BODIES - 2)


def build(nc, a, out):
    scr = {
        "xT": nc.dram_tensor("xT_parts", [B * TB, P, 2, KC, P], F32, kind="Internal").ap(),
        "k": nc.dram_tensor("k_parts", [KVH, P, 2, B * S], F32, kind="Internal").ap(),
        "v": nc.dram_tensor("v_parts", [KVH, P, 2, B * TB, DH], F32, kind="Internal").ap(),
        "ffn": nc.dram_tensor("ffn_out", [B * TB, P, D], F32, kind="Internal").ap(),
    }
    key_value_and_ffn(nc, a, scr, [])
    attention(nc, a, scr, out)


def kernel(L0_attn_hidden_states, L0_attn_Wq, L0_attn_Wkr, L0_attn_Wdk, L0_attn_Wupk, L0_attn_Wupv,
           L0_attn_Wo, L0_ffn_W_gate, L0_ffn_W_up, L0_ffn_W_down):
    import numpy as np
    import concourse.bacc as bacc
    from concourse.bass_utils import run_bass_kernel_spmd

    x, Wq, Wkr, Wdk, Wupk, Wupv, Wo, Wg, Wu, Wd = (np.asarray(v) for v in (
        L0_attn_hidden_states, L0_attn_Wq, L0_attn_Wkr, L0_attn_Wdk, L0_attn_Wupk, L0_attn_Wupv,
        L0_attn_Wo, L0_ffn_W_gate, L0_ffn_W_up, L0_ffn_W_down))

    def by_partition(wt, cols):
        k, n = wt.shape
        return wt.reshape(k // P, P, n // cols, cols).transpose(2, 1, 0, 3)

    gate, up = (by_partition(w.T, P).reshape(MB, P, C) for w in (Wg, Wu))
    inv_freq = 1.0 / 10000.0 ** (np.arange(0, DH, 2, dtype=np.float32) / DH)
    freqs = np.outer(np.arange(S, dtype=np.float32), inv_freq)
    cs = np.stack([np.cos(freqs), np.sin(freqs)], 1).astype(np.float32)
    scale = np.float32(1.0) / np.sqrt(np.float32(DH))
    arrays = {
        "x": x.reshape(CHUNKS, CT, P, D).transpose(0, 2, 1, 3),
        "wq": by_partition(Wq.T, GRP * DH),
        "wkr": by_partition(Wkr.T, 512)[0],
        "wdk": by_partition(Wdk.T, 512)[0],
        "wupk": by_partition(Wupk.T, 512)[0],
        "wupv": by_partition(Wupv.T, 512),
        "wo": Wo.T.reshape(KVH, GRP, DH, D).transpose(0, 2, 1, 3),
        "ffw": np.concatenate([gate, up, Wd.T.reshape(MB, P, D)], axis=2),
        "ktab": np.tile(cs[:, :, 0:RH].reshape(S // CHUNK, CT, P, 2, RH).transpose(0, 2, 1, 3, 4),
                        (B, 1, 1, 1, 1)),
        "qtab": (cs * scale).reshape(TB, P, 2, HALF).transpose(1, 0, 2, 3),
    }
    arrays = {k: np.ascontiguousarray(v) for k, v in arrays.items()}
    nc = bacc.Bacc("TRN2", target_bir_lowering=False, num_devices=1)
    a = {k: nc.dram_tensor(f"in_{k}", v.shape, mybir.dt.from_np(v.dtype), kind="ExternalInput").ap()
         for k, v in arrays.items()}
    out = nc.dram_tensor("out", [B, P, TB, D], F32, kind="ExternalOutput").ap()
    build(nc, a, out)
    r = run_bass_kernel_spmd(nc, [{f"in_{k}": v for k, v in arrays.items()}], core_ids=[0])
    return np.ascontiguousarray(r.results[0]["out"].transpose(0, 2, 1, 3)).reshape(B, S, D)
```

```python
from contextlib import ExitStack

import concourse.bass as bass
from concourse import mybir

F32 = mybir.dt.float32
F32R = mybir.dt.float32r
F16 = mybir.dt.float16
BF16 = mybir.dt.bfloat16
ACT = mybir.ActivationFunctionType
ALU = mybir.AluOpType
AX = mybir.AxisListType

HI, LO = 0, 1
PASSES = ((HI, HI), (HI, LO), (LO, HI))

P = 128
B, S, D = 2, 1024, 512
HEADS, KVH, DH = 32, 8, 128
GRP = HEADS // KVH
HALF = DH // 2
RH = 32
KC = D // P
C = 512
CC = C // P
M = 1792
MB = M // P
TB = S // P
CHUNK = 512
CT = CHUNK // P
CHUNKS = B * S // CHUNK
FFW = 3 * C
EPS = 1e-5
MASKED = -1e30

RING = 4
G_XT = 0
G_KR = G_XT + KC
G_CT = G_KR + CT
G_KRT = G_CT + CC
G_KN = G_KRT + KVH // 2
G_V = G_KN + KVH // 2
GROUPS = G_V + 2 * CT
STORED = range(G_KRT, GROUPS)
SPLITS = GROUPS - CT


def split_no(n):
    return n + 1 if n < G_KR else n + 1 - CT


def stores_upto(slot, n):
    return sum(4 if m < G_V else 2 for m in STORED if m % RING == slot and m <= n)


PAIRS = KVH // 2
BODIES = B * PAIRS
UNITS = 2 * TB
HPB = UNITS * GRP
EARLY = 2


def unit_kv(n):
    return n // TB


ORDER = [TB - 1 - j // 2 if j % 2 else j // 2 for j in range(TB)]


def unit_block(n):
    return ORDER[n % TB]


def key_blocks(n):
    return unit_block(n) + 1


def first_key_block(n):
    return sum(key_blocks(m) for m in range(n))


KEYB = first_key_block(UNITS)


def product_order(units):
    out = [("Q", 0, 0), ("QT", 0, 0), ("Q", 1, 0)]
    turned = []
    for k in range(units + 2):
        if k % UNITS == EARLY and k < units:
            out.append(("CUT", k - EARLY, 0))
        left = list(range(key_blocks(k - 1))) if 1 <= k <= units else []
        for what in STEP[k % 2]:
            if what == "T":
                for j in left[:1]:
                    out.append(("T", k - 1, left.pop(0)))
                    turned.append((k - 1, j))
                if len(turned) > LAG:
                    out.append(("PV", *turned.pop(0)))
            elif what == "rest":
                while left:
                    out.append(("T", k - 1, left[0]))
                    turned.append((k - 1, left.pop(0)))
                    if len(turned) > LAG:
                        out.append(("PV", *turned.pop(0)))
            elif what == "end":
                while turned and turned[0][0] < k - 1:
                    out.append(("PV", *turned.pop(0)))
            else:
                n = k + {"S": 0, "QT": 1, "Q": 2, "W": -2}[what.rstrip("0123")]
                if 0 <= n < units:
                    out.append((what.rstrip("0123"), n, int(what[-1]) if what[-1].isdigit() else 0))
    return out


STEP = (("S0", "S1", "QT", "end", "T", "T", "S2", "S3", "W", "T", "Q", "rest"),
        ("S0", "QT", "S1", "T", "end", "T", "Q", "S2", "S3", "W", "rest"))
LAG = 2
WHOLE = product_order(3 * UNITS)
MISC_NO = {e[:2]: i for i, e in enumerate(e for e in WHOLE if e[0] in ("Q", "QT", "W"))}
MPB = 3 * UNITS
Q_TO_W = 4


def is_last(kind, n, j):
    return kind == "PV" and j == key_blocks(n) - 1


def followers(kind, n, j):
    cols = key_blocks(n) * P / 1000
    if kind == "S":
        yield 0, [("dve", "S", n, j, cols + 0.1), ("act", "EXP", n, j, 0.9 * cols + 0.2),
                  ("dve", "INV", n, j, 0.1), ("pool", "NORM", n, j, 1.8 * cols + 0.1)]
    elif kind == "Q":
        yield 0, [("dve", "Q", n, j, 1.4), ("pool", "Q", n, j, 1.4)]
    elif kind == "W":
        yield 0, [("dve", "W", n, j, 0.65)]
    elif kind in ("QT", "T") or is_last(kind, n, j):
        yield 0, [("act", kind, n, j, 0.55), ("dve", kind, n, j, 0.65)]
    if kind in ("Q", "W") and (n + 1) % TB == 0:
        split = "XQ" if kind == "Q" else "XO"
        for p in range(4):
            yield SPLIT_GAP * p, [("act", split, n + 1, p, 0.6), ("dve", split, n + 1, p, 0.65)]


SPLIT_GAP = 0.7


def orders():
    cost = {"Q": 2.6, "QT": 0.44, "T": 0.44, "PV": 0.65, "W": 2.6}
    free = dict(act=0.0, dve=0.0, pool=0.0)
    ready, done, taken, early, cuts, serial, now = [], {}, {}, set(), [], 0, 0.0

    def take():
        at, _, chain = ready.pop(0)
        engine, kind, n, j, c = chain[0]
        start = max(at, free[engine])
        free[engine] = done[engine, kind, n, j] = start + c
        taken[engine, kind, n, j] = at
        if chain[1:]:
            ready.append((start + c + 0.05, len(taken) + 10 ** 6, chain[1:]))
            ready.sort()

    misc = None
    blocks = []
    for kind, n, j in product_order(4 * UNITS):
        if kind == "CUT":
            cuts.append(now)
            continue
        waits = []
        if kind in ("Q", "QT", "W"):
            waits += [misc] if misc else []
            misc = ("dve", kind, n, j)
        if kind == "Q" and n % TB == 0 and n:
            waits.append(("dve", "XQ", n, 2))
        if kind == "W":
            waits += [("dve", "PV", n, key_blocks(n) - 1)] + [("dve", "XO", n, 2)] * (n % TB == 0 and n > 0)
        if kind == "QT":
            waits.append(("pool", "Q", n, 0))
        if kind == "S":
            waits.append(("dve", "QT", n, 0))
            head = n * GRP + j - 2
            if head >= 0:
                waits.append(("act", "EXP", head // GRP, head % GRP))
        if kind == "T":
            waits.append(("pool", "NORM", n, GRP - 1))
            waits += [("dve", "T", *b) for b in blocks[-2:-1]]
            blocks.append((n, j))
        if kind == "PV":
            waits.append(("dve", "T", n, j))
        while ready and (ready[0][0] <= now or any(w not in done for w in waits)):
            take()
        for w in waits:
            now = max(now, done[w] + 0.05)
        now += 3 * key_blocks(n) * P * 0.00042 + 0.1 if kind == "S" else cost[kind]
        for gap, chain in followers(kind, n, j):
            serial += 1
            if len(cuts) <= 2:
                early.update(step[:4] for step in chain)
            ready.append((now + gap + 0.05, serial, chain))
            ready.sort()
    while ready:
        take()
    period = cuts[3] - cuts[2]
    out = {}
    for engine in free:
        times = {k[1:]: t for k, t in taken.items() if k[0] == engine}
        keyed = []
        for (kind, n, j), t in times.items():
            if UNITS <= n - UNITS < 2 * UNITS:
                for b in range(3):
                    keyed.append((round(t + (b - 2) * period, 3), (kind, n + (b - 2) * UNITS, j)))
        end = round(max(t for k, t in taken.items() if k[0] == engine and k in early), 3) + 5e-4
        keyed += [(end + (b - 2) * period, ("CUT", b * UNITS, 0)) for b in range(3)]
        out[engine] = [e for _, e in sorted(keyed)]
    return out


ORDERS = orders()


def cut(seq):
    c = [i for i, e in enumerate(seq) if e[0] == "CUT"]
    first, body, again, last = seq[:c[0]], seq[c[0] + 1:c[1]], seq[c[1] + 1:c[2]], seq[c[2] + 1:]
    assert [(k, n - UNITS, j) for k, n, j in again] == body
    return first, body, last


def key_value_and_ffn(nc, a, scr, prime):
    with ExitStack() as ctx:
        def sb(name, shape, dt=F32):
            return ctx.enter_context(nc.sbuf_tensor(name, shape, dt))

        def bank(name):
            return ctx.enter_context(nc.psum_tensor(name, [P, 512], F32))

        def sem(name):
            return ctx.enter_context(nc.semaphore(name))

        ident = sb("ident1", [P, P])
        w_raw = sb("w_raw", [P, 4, 512])
        w_raw2 = sb("w_raw2", [P, 4, 512])
        ff_out = w_raw
        wdk = sb("wdk", [P, 2, KC, C], F32R)
        wkr = sb("wkr", [P, 2, KC, 512], F32R)
        wupk = sb("wupk", [P, 2, CC, 512], F32R)
        wupv = sb("wupv", [P, 2, 2, CC, 512], F32R)
        ktab = sb("ktab", [P, CT, 2, RH])
        x_in = sb("x_in", [P, CT, D])
        xn = sb("xn", [P, CT, D])
        stats = sb("stats", [P, CT, 6])
        mv = sb("mv", [P, CT, 2])
        var_eps = sb("var_eps", [P, CT])
        power = sb("power", [P, CT])
        rstd = sb("rstd", [P, CT])
        xT = sb("xT1", [P, 2, KC, CHUNK], F32R)
        cT = sb("cT", [P, 2, CC, CHUNK], F32R)
        k_cos = sb("k_cos", [P, 512])
        k_sin = sb("k_sin", [P, 512])
        k_rot = sb("k_rot", [P, CT, 512])
        stage = sb("stage", [P, RING, 2, 512], F32R)
        ff_raw = sb("ff_raw", [P, 2, FFW], F16)
        ff_w = sb("ff_w", [P, 2, FFW], F32R)
        silu = sb("silu", [P, 512])
        h32 = sb("h32", [P, 512])
        hT = sb("hT", [P, 2, 2, 512], F32R)
        ring = [bank(f"ring{i}") for i in range(RING)]
        down = [bank(f"down{i}") for i in range(CT)]

        ident_ready = sem("ident_ready")
        w_loaded = [sem(f"w_loaded{i}") for i in range(5)]
        w_hi = sem("w_hi")
        w_split = sem("w_split")
        x_loaded = sem("x_loaded")
        tab_loaded = sem("tab_loaded")
        ln_step = sem("ln_step")
        rstd_ready = sem("rstd_ready")
        xn_ready = sem("xn_ready")
        group_done = sem("group_done")
        hi_ready = sem("hi_ready")
        emptied = sem("emptied")
        rotated = sem("rotated")
        stored = [sem(f"stored{i}") for i in range(RING)]
        xT_stored = sem("xT_stored")
        ff_loaded = [sem(f"ff_loaded{i}") for i in range(2)]
        gate_up_cast = sem("gate_up_cast")
        down_cast = sem("down_cast")
        gate_done = sem("gate_done")
        up_done = sem("up_done")
        res_loaded = sem("res_loaded")
        silu_ready = sem("silu_ready")
        h_ready = sem("h_ready")
        h_hi = sem("h_hi")
        h_split = sem("h_split")
        down_done = sem("down_done")
        ff_copied = sem("ff_copied")
        ff_stored = sem("ff_stored")

        prime += [(group_done, GROUPS), (hi_ready, SPLITS), (emptied, GROUPS), (rotated, CT),
                  (xn_ready, CT), (xT_stored, 16 * CT), (gate_up_cast, MB), (down_cast, MB), (gate_done, MB),
                  (up_done, MB), (silu_ready, MB), (h_ready, MB), (h_hi, MB), (h_split, MB),
                  (down_done, MB), (ff_copied, CT), (x_loaded, 16), (tab_loaded, 16),
                  (ff_loaded[0], 16 * MB // 2), (ff_loaded[1], 16 * MB // 2),
                  (ff_stored, 16),
                  (ln_step, 2), (rstd_ready, 1)]
        prime += [(stored[s], 16 * stores_upto(s, GROUPS)) for s in range(RING)]
        with nc.Block() as start:
            @start.sync
            def _(sp):
                for s, n in prime:
                    sp.sem_inc(s, n)

        weights = [(a["wkr"], wkr), (a["wdk"], wdk), (a["wupk"], wupk)]
        weights = [(src, dst[:, HI], dst[:, LO]) for src, dst in weights]
        weights += [(a["wupv"][v], wupv[:, HI, v], wupv[:, LO, v]) for v in range(2)]
        raw = [w_raw, k_rot, w_raw2, w_raw, w_raw2]
        split_ahead = {G_XT: (0,), G_KR: (1,), G_CT: (2,), G_KRT: (3, 4)}
        block = ctx.enter_context(nc.Block())

        @block.sync
        def _(sp):
            def load_x(c):
                sp.wait_ge(xn_ready, (c + 1) * CT)
                sp.dma_start(x_in[:], a["x"][c]).then_inc(x_loaded, 16)
                sp.wait_ge(emptied, c * GROUPS + G_CT)
                sp.dma_start(ktab[:], a["ktab"][c]).then_inc(tab_loaded, 16)

            def load_ff(c1, m, o):
                sp.wait_ge(down_cast, c1 * MB + m - 1)
                sp.dma_start(ff_raw[:, o], a["ffw"][m]).then_inc(ff_loaded[o], 16)

            def chunk(c, last=False):
                c1 = c + 1
                sp.wait_ge(emptied, c1 * GROUPS + G_KR)
                for t in range(CT):
                    sp.dma_start(scr["xT"][c * CT + t].rearrange("p a k s -> p (a k) s"),
                                 xT[:, :, :, t * P:(t + 1) * P].bitcast(F32)
                                 .rearrange("p a k s -> p (a k) s")).then_inc(xT_stored, 16)
                load_ff(c1, 0, 0)
                load_ff(c1, 1, 1)
                if not last:
                    load_x(c + 1)
                for n in STORED:
                    s = n % RING
                    sp.wait_ge(emptied, c1 * GROUPS + n + 1)
                    if n < G_V:
                        pair, low = (n - G_KRT, 0) if n < G_KN else (n - G_KN, RH)
                        for q in range(4):
                            row = (q % 2) * HALF + low
                            sp.dma_start(scr["k"][2 * pair + q // 2, row:row + RH, :,
                                                  bass.ds(c * CHUNK, CHUNK)],
                                         stage[q * RH:(q + 1) * RH, s].bitcast(F32))\
                                .then_inc(stored[s], 16)
                    else:
                        t, v = (n - G_V) // 2, (n - G_V) % 2
                        for part in (HI, LO):
                            sp.dma_start(
                                scr["v"][v * 4:v * 4 + 4, :, part, c * CT + t, :]
                                .rearrange("g p d -> p g d"),
                                stage[:, s, part].bitcast(F32).rearrange("p (g d) -> p g d", g=4))\
                                .then_inc(stored[s], 16)
                sp.wait_ge(w_split, len(weights))
                sp.wait_ge(ff_stored, c1 * 16)
                sp.dma_start(ff_out[:], a["x"][c]).then_inc(res_loaded, 16)
                with sp.Fori(1, MB // 2) as m2:
                    for o in range(2):
                        load_ff(c1, m2 * 2 + o, o)

            load_x(0)
            for n, (src, _, _) in enumerate(weights):
                if n > 2:
                    sp.wait_ge(w_split, (n - 3) * 2 + 1)
                sp.dma_start(raw[n][:], src).then_inc(w_loaded[n], 16)
            with sp.Fori(0, CHUNKS - 1) as c:
                chunk(c)
            chunk(CHUNKS - 1, last=True)
            sp.wait_ge(xT_stored, 16 * CT * (CHUNKS + 1))
            for s in range(RING):
                sp.wait_ge(stored[s], 16 * stores_upto(s, GROUPS) * (CHUNKS + 1))
            sp.wait_ge(ff_stored, 16 * (CHUNKS + 1))

        @block.gpsimd
        def _(pool):
            nc.gpsimd.memset(power[:], -0.5).then_inc(ident_ready, 1)
            nc.gpsimd.memset(ident[:], 0.0).then_inc(ident_ready, 1)
            pool.wait_ge(ident_ready, 2)
            nc.gpsimd.affine_select(out=ident[:], in_=ident[:], compare_op=ALU.not_equal, fill=1.0,
                                    base=0, pattern=[[-1, P]], channel_multiplier=1)\
                .then_inc(ident_ready, 1)

            def rstd_of(c1):
                pool.wait_ge(ln_step, c1 * 2 + 2)
                nc.gpsimd.tensor_tensor(rstd[:], var_eps[:], power[:], ALU.pow).then_inc(rstd_ready, 1)

            def rotate(c1):
                for t in range(CT):
                    kc, ks, kr = (v.rearrange("p (g h r) -> p g h r", h=2, r=RH)
                                  for v in (k_cos[:], k_sin[:], k_rot[:, t]))
                    pool.wait_ge(emptied, c1 * GROUPS + G_KR + t + 1)
                    nc.gpsimd.tensor_tensor(kr[:, :, 0], kc[:, :, 0], ks[:, :, 0], ALU.subtract)
                    nc.gpsimd.tensor_tensor(kr[:, :, 1], kc[:, :, 1], ks[:, :, 1], ALU.add)\
                        .then_inc(rotated, 1)

            rstd_of(1)
            pool.wait_ge(w_split, 2)
            with pool.Fori(0, CHUNKS - 1) as c:
                rotate(c + 1)
                rstd_of(c + 2)
            rotate(CHUNKS)

        @block.scalar
        def _(act):
            def split_weights(ns):
                for n in ns:
                    act.wait_ge(w_loaded[n], 16)
                    nc.scalar.activation(weights[n][1], raw[n][:], ACT.Copy).then_inc(w_hi, 1)

            def cast_gate_up(c1, m, o):
                act.wait_ge(ff_loaded[o], (c1 * MB + m + (2 - o)) * 8)
                act.wait_ge(up_done, c1 * MB + m - 1)
                nc.scalar.activation(ff_w[:, o, 0:2 * C], ff_raw[:, o, 0:2 * C], ACT.Copy)\
                    .then_inc(gate_up_cast, 1)

            def cast_down(c1, m, o):
                act.wait_ge(down_done, c1 * MB + m - 1)
                nc.scalar.activation(ff_w[:, o, 2 * C:], ff_raw[:, o, 2 * C:], ACT.Copy)\
                    .then_inc(down_cast, 1)

            def gate(c1, m, o):
                act.wait_ge(gate_done, c1 * MB + m + 1)
                act.wait_ge(h_ready, c1 * MB + m)
                nc.scalar.activation(silu[:], ring[o][:], ACT.Silu).then_inc(silu_ready, 1)
                act.wait_ge(h_ready, c1 * MB + m + 1)
                act.wait_ge(down_done, c1 * MB + m - 1)
                nc.scalar.activation(hT[:, o, HI], h32[:], ACT.Copy).then_inc(h_hi, 1)

            def chunk(c1, first=False):
                for n in range(G_XT, GROUPS):
                    if first:
                        split_weights(split_ahead.get(n, ()))
                    if n == G_KR and not first:
                        store_ff(c1 - 1)
                    if n == G_V:
                        cast_gate_up(c1, 0, 0)
                    if n == G_V + 2:
                        cast_gate_up(c1, 1, 1)
                    if n == G_V + 4:
                        cast_down(c1, 0, 0)
                    if G_KR <= n < G_CT:
                        continue
                    act.wait_ge(group_done, c1 * GROUPS + n + 1)
                    if n < G_KR:
                        if n == 0:
                            act.wait_ge(xT_stored, c1 * (16 * CT))
                        dst = xT[:, HI, n - G_XT]
                    elif n < G_KRT:
                        dst = cT[:, HI, n - G_CT]
                    else:
                        s = n % RING
                        act.wait_ge(stored[s], c1 * (16 * stores_upto(s, GROUPS)) + 16 * stores_upto(s, n - 1))
                        dst = stage[:, s, HI]
                    nc.scalar.activation(dst, ring[n % RING][:], ACT.Copy).then_inc(hi_ready, 1)
                with act.Fori(0, MB // 2 - 1) as m2:
                    for o in range(2):
                        gate(c1, m2 * 2 + o, o)
                        cast_gate_up(c1, m2 * 2 + (o + 2), o)
                        cast_down(c1, m2 * 2 + (o + 1), 1 - o)
                gate(c1, MB - 2, 0)
                cast_down(c1, MB - 1, 1)
                gate(c1, MB - 1, 1)

            def store_ff(c1):
                act.wait_ge(ff_copied, c1 * CT + CT)
                act.dma_start(scr["ffn"][bass.ds(c1 * CT - CT, CT)].rearrange("t p d -> p t d"), ff_out[:])\
                    .then_inc(ff_stored, 16)

            chunk(1, first=True)
            with act.Fori(1, CHUNKS) as c:
                chunk(c + 1)
            store_ff(CHUNKS)

        @block.vector
        def _(dve):
            def split_weights(ns):
                for n in ns:
                    _, hi, lo = weights[n]
                    dve.wait_ge(w_hi, n + 1)
                    nc.vector.tensor_tensor(lo, raw[n][:], hi.bitcast(F32), ALU.subtract).then_inc(w_split, 1)

            def split_lo(c1, n, hi, lo):
                dve.wait_ge(hi_ready, c1 * SPLITS + split_no(n))
                nc.vector.tensor_tensor(lo, ring[n % RING][:], hi.bitcast(F32), ALU.subtract)\
                    .then_inc(emptied, 1)

            def hidden(c1, m, o):
                dve.wait_ge(up_done, c1 * MB + m + 1)
                dve.wait_ge(silu_ready, c1 * MB + m + 1)
                dve.wait_ge(h_split, c1 * MB + m)
                nc.vector.tensor_tensor(h32[:], ring[2 + o][:], silu[:], ALU.mult).then_inc(h_ready, 1)
                dve.wait_ge(h_hi, c1 * MB + m + 1)
                nc.vector.tensor_tensor(hT[:, o, LO], h32[:], hT[:, o, HI].bitcast(F32), ALU.subtract)\
                    .then_inc(h_split, 1)

            def layer_norm(c1):
                dve.wait_ge(x_loaded, c1 * 16 + 16)
                for t in range(CT):
                    nc.vector.bn_stats(stats[:, t], x_in[:, t])
                dve.drain()
                for t in range(CT):
                    ins = nc.vector.bn_aggr(mv[:, t], stats[:, t])
                ins.then_inc(ln_step, 1)
                dve.wait_ge(ln_step, c1 * 2 + 1)
                nc.vector.tensor_scalar(var_eps[:], mv[:, :, 1], EPS, None, ALU.add).then_inc(ln_step, 1)
                dve.wait_ge(rstd_ready, c1 + 1)
                dve.wait_ge(group_done, c1 * GROUPS - GROUPS + G_KR)
                for t in range(CT):
                    nc.vector.tensor_scalar(xn[:, t], x_in[:, t], mv[:, t, 0:1], rstd[:, t:t + 1],
                                            ALU.subtract, ALU.mult).then_inc(xn_ready, 1)

            def projections(c1, first=False):
                for n in range(G_XT, GROUPS):
                    if first:
                        split_weights(split_ahead.get(n, ()))
                    elif n == G_KR:
                        finish_ffn(c1 - 1)
                    if n < G_KR:
                        split_lo(c1, n, xT[:, HI, n - G_XT], xT[:, LO, n - G_XT])
                    elif n < G_CT:
                        turn_keys(c1, n)
                    else:
                        dst = cT[:, :, n - G_CT] if n < G_KRT else stage[:, n % RING]
                        split_lo(c1, n, dst[:, HI], dst[:, LO])

            def turn_keys(c1, n):
                t = n - G_KR
                k, kc, ks = (v.rearrange("p (g h r) -> p g h r", h=2, r=RH)
                             for v in (ring[n % RING][:], k_cos[:], k_sin[:]))
                cos, sin = (ktab[:, t, i].unsqueeze(1).broadcast_to([P, KVH, RH]) for i in range(2))
                if t == 0:
                    dve.wait_ge(tab_loaded, c1 * 16 + 16)
                dve.wait_ge(group_done, c1 * GROUPS + n + 1)
                dve.wait_ge(rotated, c1 * CT + t)
                for h in range(2):
                    nc.vector.tensor_tensor(kc[:, :, h], k[:, :, h], cos, ALU.mult)
                nc.vector.tensor_tensor(ks[:, :, 0], k[:, :, 1], sin, ALU.mult)
                nc.vector.tensor_tensor(ks[:, :, 1], k[:, :, 0], sin, ALU.mult).then_inc(emptied, 1)

            def ffn(c1):
                with dve.Fori(0, MB // 2) as m2:
                    for o in range(2):
                        hidden(c1, m2 * 2 + o, o)

            def finish_ffn(c1):
                dve.wait_ge(down_done, c1 * MB + MB)
                dve.wait_ge(res_loaded, c1 * 16)
                for t in range(CT):
                    nc.vector.tensor_tensor(ff_out[:, t], down[t][:], ff_out[:, t], ALU.add)\
                        .then_inc(ff_copied, 1)

            layer_norm(1)
            projections(1, first=True)
            layer_norm(2)
            ffn(1)
            with dve.Fori(1, CHUNKS - 1) as c:
                projections(c + 1)
                layer_norm(c + 2)
                ffn(c + 1)
            projections(CHUNKS)
            ffn(CHUNKS)
            finish_ffn(CHUNKS)

        @block.tensor
        def _(pe):
            def products(n, c1, pairs, out=None):
                pe.wait_ge(emptied, c1 * GROUPS + n + 1 - RING)
                for i, (l, r) in enumerate(pairs):
                    mm = nc.tensor.matmul(ring[n % RING][:], l, r, start=(i == 0), stop=(i == len(pairs) - 1))
                mm.then_inc(group_done, 1)

            def transposes(n, c1, blocks):
                pe.wait_ge(emptied, c1 * GROUPS + n + 1 - RING)
                for i, src in enumerate(blocks):
                    mm = nc.tensor.transpose(ring[n % RING][:, i * P:(i + 1) * P], src, ident[:])
                mm.then_inc(group_done, 1)

            def gate_up(c1, m, o):
                pe.wait_ge(gate_up_cast, c1 * MB + m + 1)
                pe.wait_ge(h_ready, c1 * MB + m - 1)
                for side, done in ((0, gate_done), (1, up_done)):
                    w = ff_w[:, o, side * C:(side + 1) * C]
                    for i in range(2 * KC):
                        mm = nc.tensor.matmul(ring[2 * side + o][:], w[:, (i // 2) * P:(i // 2 + 1) * P],
                                              xT[:, i % 2, i // 2], start=(i == 0), stop=(i == 2 * KC - 1))
                    mm.then_inc(done, 1)

            def project_down(c1, m, o, first=False, last=False):
                pe.wait_ge(down_cast, c1 * MB + m + 1)
                pe.wait_ge(h_split, c1 * MB + m + 1)
                for t in range(CT):
                    for part in (HI, LO):
                        mm = nc.tensor.matmul(down[t][:], hT[:, o, part, t * P:(t + 1) * P],
                                              ff_w[:, o, 2 * C:3 * C],
                                              start=(first and part == HI), stop=(last and part == LO))
                mm.then_inc(down_done, 1)

            pe.wait_ge(ident_ready, 3)
            with pe.Fori(0, CHUNKS) as c:
                c1 = c + 1
                pe.wait_ge(xn_ready, c1 * CT + CT)
                pe.wait_ge(h_ready, c1 * MB)
                for k in range(KC):
                    transposes(G_XT + k, c1, [xn[:, t, k * P:(k + 1) * P] for t in range(CT)])
                pe.wait_ge(emptied, c1 * GROUPS + G_KR)
                pe.wait_ge(w_split, 1)
                for t in range(CT):
                    products(G_KR + t, c1, [(xT[:, x, k, t * P:(t + 1) * P], wkr[:, w, k])
                                            for k in range(KC) for x, w in PASSES])
                pe.wait_ge(w_split, 2)
                for m in range(CC):
                    products(G_CT + m, c1, [(wdk[:, w, k, m * P:(m + 1) * P], xT[:, x, k])
                                            for k in range(KC) for w, x in PASSES])
                pe.wait_ge(rotated, c1 * CT + CT)
                for q in range(KVH // 2):
                    transposes(G_KRT + q, c1, [k_rot[:, t, q * P:(q + 1) * P] for t in range(CT)])
                pe.wait_ge(emptied, c1 * GROUPS + G_KRT)
                pe.wait_ge(w_split, len(weights))
                for q in range(KVH // 2):
                    products(G_KN + q, c1, [(wupk[:, w, k, q * P:(q + 1) * P], cT[:, x, k])
                                            for k in range(CC) for w, x in PASSES])
                for t in range(CT):
                    for v in range(2):
                        products(G_V + 2 * t + v, c1, [(cT[:, x, k, t * P:(t + 1) * P], wupv[:, w, v, k])
                                                       for k in range(CC) for x, w in PASSES])
                pe.wait_ge(emptied, c1 * GROUPS + GROUPS)
                gate_up(c1, 0, 0)
                gate_up(c1, 1, 1)
                pe.wait_ge(ff_copied, c1 * CT)
                project_down(c1, 0, 0, first=True)
                with pe.Fori(0, MB // 2 - 1) as m2:
                    gate_up(c1, m2 * 2 + 2, 0)
                    project_down(c1, m2 * 2 + 1, 1)
                    gate_up(c1, m2 * 2 + 3, 1)
                    project_down(c1, m2 * 2 + 2, 0)
                project_down(c1, MB - 1, 1, last=True)


def attention(nc, a, scr, out):
    with ExitStack() as ctx:
        def sb(name, shape, dt=F32):
            return ctx.enter_context(nc.sbuf_tensor(name, shape, dt))

        def bank(name, n=1):
            return ctx.enter_context(nc.psum_tensor(name, [P, n * 512], F32))

        def sem(name):
            return ctx.enter_context(nc.semaphore(name))

        ident = sb("ident2", [P, P])
        identb = sb("identb", [P, P], BF16)
        mask = sb("mask", [P, P], BF16)
        qtab = sb("qtab", [P, TB, 2, HALF])
        xT = sb("xT2", [P, TB, 2, KC, P], F32R)
        acc = sb("acc", [P, TB, D])
        kT = sb("kT", [P, 2, 2, S], F32R)
        v_sb = sb("v_sb", [P, 2, 2, TB, DH], F32R)
        wq_raw = sb("wq_raw", [P, KC, GRP * DH])
        wq = sb("wq", [P, 2, KC, GRP * DH], F32R)
        wo_raw = sb("wo_raw", [P, GRP, D])
        wo = sb("wo", [P, 2, GRP, D], F32R)
        q_cos = sb("q_cos", [P, 512])
        q_sin = sb("q_sin", [P, 512])
        q_rot = sb("q_rot", [P, 512])
        qT = sb("qT", [P, 2, 2, 512], F32R)
        prob = sb("prob", [P, 2, GRP, S])
        pT = sb("pT", [P, 4, 2, 512], F32R)
        oT = sb("oT", [P, 2, 2, 512], F32R)
        nmax = sb("nmax", [P, 8])
        rsum = sb("rsum", [P, 8])
        rinv = sb("rinv", [P, 8])
        scores = [bank(f"scores{i}", 2) for i in range(2)]
        ptb = [bank(f"ptb{i}") for i in range(2)]
        ob = bank("ob")
        misc = bank("misc")

        const = sem("const")
        tab2 = sem("tab2")
        x_ready = [sem(f"x_ready{i}") for i in range(TB)]
        acc_ready = [sem(f"acc_ready{i}") for i in range(TB)]
        k_loaded = [sem(f"k_loaded{e}") for e in range(2)]
        v_loaded = [sem(f"v_loaded{e}") for e in range(2)]
        wq_loaded = sem("wq_loaded")
        wq_hi = sem("wq_hi")
        wq_split = sem("wq_split")
        wo_loaded = sem("wo_loaded")
        wo_hi = sem("wo_hi")
        wo_split = sem("wo_split")
        misc_done = sem("misc_done")
        misc_empty = sem("misc_empty")
        q_turned = sem("q_turned")
        qT_hi = sem("qT_hi")
        s_done = sem("s_done")
        max_ready = sem("max_ready")
        exp_done = sem("exp_done")
        inv_ready = sem("inv_ready")
        normed = sem("normed")
        t_done = sem("t_done")
        pT_hi = sem("pT_hi")
        pT_split = sem("pT_split")
        o_done = sem("o_done")
        oT_hi = sem("oT_hi")
        o_split = sem("o_split")
        stored = sem("out_stored")

        start_counts = [(misc_done, MPB), (misc_empty, MPB), (q_turned, UNITS),
                        (qT_hi, UNITS), (s_done, HPB), (max_ready, HPB), (exp_done, HPB),
                        (inv_ready, HPB), (normed, HPB), (t_done, KEYB), (pT_hi, KEYB),
                        (pT_split, KEYB), (o_done, UNITS), (oT_hi, UNITS), (o_split, UNITS),
                        (wq_loaded, 32), (wq_hi, 2 * KC), (wq_split, 2 * KC), (wo_loaded, 32),
                        (wo_hi, 2 * GRP), (wo_split, 2 * GRP), (k_loaded[0], 16),
                        (k_loaded[1], 16), (v_loaded[0], 16), (v_loaded[1], 16)]
        with nc.Block() as start:
            @start.sync
            def _(sp):
                for s, n in start_counts:
                    sp.sem_inc(s, n)

        block = ctx.enter_context(nc.Block())

        def misc_no(kind, n):
            return MISC_NO[(kind, n)]

        @block.sync
        def _(sp):
            def head_loads(b, pair, e, first=False):
                it1 = b * PAIRS + pair + 1
                sp.wait_ge(wq_split, it1 * (2 * KC) + e * KC)
                sp.dma_start(wq_raw[:], a["wq"][pair * 2 + e]).then_inc(wq_loaded, 16)
                if first:
                    load_x(b, ORDER[0])
                    load_x(b, ORDER[1])
                sp.wait_ge(s_done, it1 * HPB - (1 - e) * (HPB // 2))
                sp.dma_start(kT[:, e].bitcast(F32), scr["k"][pair * 2 + e, :, :, bass.ds(b * S, S)]).then_inc(k_loaded[e], 16)
                sp.wait_ge(o_done, it1 * UNITS - (1 - e) * TB)
                sp.dma_start(v_sb[:, e].bitcast(F32), scr["v"][pair * 2 + e, :, :, bass.ds(b * TB, TB)]).then_inc(v_loaded[e], 16)
                sp.wait_ge(wo_split, it1 * (2 * GRP) + e * GRP)
                sp.dma_start(wo_raw[:], a["wo"][pair * 2 + e]).then_inc(wo_loaded, 16)

            def load_x(b, i):
                sp.dma_start(xT[:, i].bitcast(F32), scr["xT"][b * TB + i]).then_inc(x_ready[i], 16)

            def load_acc(b, i):
                sp.dma_start(acc[:, i], scr["ffn"][b * TB + i]).then_inc(acc_ready[i], 16)

            def store_out(b, i, it1, n):
                sp.wait_ge(misc_empty, it1 * MPB + misc_no("W", n) + 1)
                sp.dma_start(out[b, :, i], acc[:, i]).then_inc(stored, 16)

            def later_pairs(b):
                with sp.Fori(1, PAIRS) as pair:
                    head_loads(b, pair, 0)
                    for ready in (x_ready, acc_ready):
                        for i in range(TB):
                            sp.wait_ge(ready[i], (b * PAIRS + pair) * 16)
                            sp.sem_inc(ready[i], 16)
                    head_loads(b, pair, 1)

            sp.dma_start(qtab[:], a["qtab"]).then_inc(tab2, 16)
            head_loads(0, 0, 0, first=True)
            for i in ORDER[2:]:
                load_x(0, i)
            for i in ORDER:
                load_acc(0, i)
            head_loads(0, 0, 1)
            later_pairs(0)
            with sp.Fori(1, B) as b:
                head_loads(b, 0, 0)
                for k in range(TB + Q_TO_W):
                    if k < TB:
                        sp.wait_ge(misc_done, b * (PAIRS * MPB) + misc_no("Q", TB + k) + 1)
                        load_x(b, ORDER[k])
                    if k >= Q_TO_W:
                        n = TB + k - Q_TO_W
                        store_out(b - 1, unit_block(n), b * PAIRS, n)
                        sp.wait_ge(stored, b * (16 * TB) - 16 * (UNITS - 1 - n))
                        load_acc(b, unit_block(n))
                head_loads(b, 0, 1)
                later_pairs(b)
            for n in range(3 * UNITS - TB, 3 * UNITS):
                store_out(B - 1, unit_block(n), BODIES - 2, n)
            sp.wait_ge(stored, 16 * B * TB)

        @block.gpsimd
        def _(pool):
            nc.gpsimd.memset(ident[:], 0.0).then_inc(const, 1)
            nc.gpsimd.memset(identb[:], 0.0).then_inc(const, 1)
            nc.gpsimd.memset(mask[:], 0.0).then_inc(const, 1)
            pool.wait_ge(const, 3)
            for m in (ident, identb):
                nc.gpsimd.affine_select(out=m[:], in_=m[:], compare_op=ALU.not_equal, fill=1.0,
                                        base=0, pattern=[[-1, P]], channel_multiplier=1).then_inc(const, 1)
            nc.gpsimd.affine_select(out=mask[:], in_=mask[:], compare_op=ALU.is_ge, fill=MASKED,
                                    base=0, pattern=[[-1, P]], channel_multiplier=1).then_inc(const, 1)

            def work(events, it1):
                for kind, n, h in events:
                    if kind == "NORM":
                        hd, W = n * GRP + h, key_blocks(n) * P
                        pool.wait_ge(inv_ready, it1 * HPB + hd + 1)
                        nc.gpsimd.tensor_tensor(prob[:, n % 2, h, 0:W], prob[:, n % 2, h, 0:W],
                                                rinv[:, hd % 8:hd % 8 + 1].broadcast_to([P, W]), ALU.mult)\
                            .then_inc(normed, 1)
                    elif kind == "Q":
                        qc, qs, qr = (v.rearrange("p (h f r) -> p h f r", f=2, r=HALF)
                                      for v in (q_cos[:], q_sin[:], q_rot[:]))
                        pool.wait_ge(misc_empty, it1 * MPB + misc_no("Q", n) + 1)
                        if n:
                            pool.wait_ge(misc_done, it1 * MPB + misc_no("QT", n - 1) + 1)
                        nc.gpsimd.tensor_tensor(qr[:, :, 0], qc[:, :, 0], qs[:, :, 0], ALU.subtract)
                        nc.gpsimd.tensor_tensor(qr[:, :, 1], qc[:, :, 1], qs[:, :, 1], ALU.add)\
                            .then_inc(q_turned, 1)

            first, body, last = cut(ORDERS["pool"])
            work(first, 1)
            with pool.Fori(0, BODIES - 1) as it:
                work(body, it + 1)
            work(last, BODIES - 2)

        @block.scalar
        def _(act):
            def work(events, it1):
                for kind, n, j in events:
                    if kind == "EXP":
                        hd, W = n * GRP + j, key_blocks(n) * P
                        act.wait_ge(max_ready, it1 * HPB + hd + 1)
                        act.wait_ge(inv_ready, it1 * HPB + hd - 7)
                        nc.scalar.activation(prob[:, n % 2, j, 0:W], scores[hd % 2][:, 0:W], ACT.Exp,
                                             bias=nmax[:, hd % 8:hd % 8 + 1],
                                             accum_out=rsum[:, hd % 8:hd % 8 + 1]).then_inc(exp_done, 1)
                    elif kind == "QT":
                        act.wait_ge(misc_done, it1 * MPB + misc_no("QT", n) + 1)
                        nc.scalar.activation(qT[:, n % 2, HI], misc[:], ACT.Copy).then_inc(qT_hi, 1)
                    elif kind == "T":
                        t = first_key_block(n) + j
                        act.wait_ge(t_done, it1 * KEYB + t + 1)
                        nc.scalar.activation(pT[:, t % 4, HI], ptb[t % 2][:], ACT.Copy).then_inc(pT_hi, 1)
                    elif is_last(kind, n, j):
                        act.wait_ge(o_done, it1 * UNITS + n + 1)
                        nc.scalar.activation(oT[:, n % 2, HI], ob[:], ACT.Copy).then_inc(oT_hi, 1)
                    elif kind == "XQ":
                        if j == 0:
                            if n:
                                act.wait_ge(misc_done, it1 * MPB + misc_no("Q", n - 1) + 1)
                            act.wait_ge(wq_loaded, (it1 * 2 + unit_kv(n) + 1) * 16)
                        nc.scalar.activation(wq[:, HI, j], wq_raw[:, j], ACT.Copy).then_inc(wq_hi, 1)
                    elif kind == "XO":
                        if j == 0:
                            if n:
                                act.wait_ge(misc_done, it1 * MPB + misc_no("W", n - 1) + 1)
                            act.wait_ge(wo_loaded, (it1 * 2 + unit_kv(n) + 1) * 16)
                        nc.scalar.activation(wo[:, HI, j], wo_raw[:, j], ACT.Copy).then_inc(wo_hi, 1)

            first, body, last = cut(ORDERS["act"])
            act.wait_ge(const, 6)
            work(first, 1)
            with act.Fori(0, BODIES - 1) as it:
                work(body, it + 1)
            work(last, BODIES - 2)

        @block.vector
        def _(dve):
            def work(events, it1):
                for kind, n, j in events:
                    if kind == "S":
                        hd, W = n * GRP + j, key_blocks(n) * P
                        dve.wait_ge(s_done, it1 * HPB + hd + 1)
                        dve.wait_ge(exp_done, it1 * HPB + hd - 7)
                        nc.vector.tensor_reduce(nmax[:, hd % 8:hd % 8 + 1], scores[hd % 2][:, 0:W],
                                                AX.X, ALU.max, negate=True).then_inc(max_ready, 1)
                    elif kind == "Q":
                        q, qc, qs = (v.rearrange("p (h f r) -> p h f r", f=2, r=HALF)
                                     for v in (misc[:], q_cos[:], q_sin[:]))
                        cos, sin = (qtab[:, unit_block(n), x].unsqueeze(1).broadcast_to([P, GRP, HALF])
                                    for x in range(2))
                        dve.wait_ge(misc_done, it1 * MPB + misc_no("Q", n) + 1)
                        dve.wait_ge(q_turned, it1 * UNITS + n)
                        for f in range(2):
                            nc.vector.tensor_tensor(qc[:, :, f], q[:, :, f], cos, ALU.mult)
                        nc.vector.tensor_tensor(qs[:, :, 0], q[:, :, 1], sin, ALU.mult)
                        nc.vector.tensor_tensor(qs[:, :, 1], q[:, :, 0], sin, ALU.mult)\
                            .then_inc(misc_empty, 1)
                    elif kind == "QT":
                        dve.wait_ge(qT_hi, it1 * UNITS + n + 1)
                        nc.vector.tensor_tensor(qT[:, n % 2, LO], misc[:], qT[:, n % 2, HI].bitcast(F32),
                                                ALU.subtract).then_inc(misc_empty, 1)
                    elif kind == "T":
                        t = first_key_block(n) + j
                        dve.wait_ge(pT_hi, it1 * KEYB + t + 1)
                        nc.vector.tensor_tensor(pT[:, t % 4, LO], ptb[t % 2][:], pT[:, t % 4, HI].bitcast(F32),
                                                ALU.subtract).then_inc(pT_split, 1)
                    elif is_last(kind, n, j):
                        dve.wait_ge(oT_hi, it1 * UNITS + n + 1)
                        nc.vector.tensor_tensor(oT[:, n % 2, LO], ob[:], oT[:, n % 2, HI].bitcast(F32),
                                                ALU.subtract).then_inc(o_split, 1)
                    elif kind == "W":
                        i_b = unit_block(n)
                        if n % UNITS < TB:
                            dve.wait_ge(acc_ready[i_b], (it1 + n // UNITS) * 16)
                        dve.wait_ge(misc_done, it1 * MPB + misc_no("W", n) + 1)
                        nc.vector.tensor_tensor(acc[:, i_b], misc[:], acc[:, i_b], ALU.add)\
                            .then_inc(misc_empty, 1)
                    elif kind == "INV":
                        hd = n * GRP + j
                        dve.wait_ge(exp_done, it1 * HPB + hd + 1)
                        dve.wait_ge(normed, it1 * HPB + hd - 7)
                        nc.vector.reciprocal(rinv[:, hd % 8:hd % 8 + 1], rsum[:, hd % 8:hd % 8 + 1])\
                            .then_inc(inv_ready, 1)
                    elif kind == "XQ":
                        dve.wait_ge(wq_hi, (it1 * 2 + unit_kv(n)) * KC + j + 1)
                        nc.vector.tensor_tensor(wq[:, LO, j], wq_raw[:, j], wq[:, HI, j].bitcast(F32),
                                                ALU.subtract).then_inc(wq_split, 1)
                    elif kind == "XO":
                        dve.wait_ge(wo_hi, (it1 * 2 + unit_kv(n)) * GRP + j + 1)
                        nc.vector.tensor_tensor(wo[:, LO, j], wo_raw[:, j], wo[:, HI, j].bitcast(F32),
                                                ALU.subtract).then_inc(wo_split, 1)

            first, body, last = cut(ORDERS["dve"])
            dve.wait_ge(tab2, 16)
            work(first, 1)
            with dve.Fori(0, BODIES - 1) as it:
                work(body, it + 1)
            work(last, BODIES - 2)

        @block.tensor
        def _(pe):
            def work(events, it1):
                for kind, n, j in events:
                    e, i, u = unit_kv(n), unit_block(n), n % 2
                    if kind in ("Q", "QT", "W"):
                        pe.wait_ge(misc_empty, it1 * MPB + misc_no(kind, n))
                    if kind == "Q":
                        if n % UNITS < TB:
                            pe.wait_ge(x_ready[i], (it1 + n // UNITS) * 16)
                        for k in range(KC):
                            if n % TB == 0:
                                pe.wait_ge(wq_split, (it1 * 2 + e) * KC + k + 1)
                            for m, (x, w) in enumerate(PASSES):
                                mm = nc.tensor.matmul(misc[:], xT[:, i, x, k], wq[:, w, k],
                                                      start=(k == 0 and m == 0),
                                                      stop=(k == KC - 1 and m == len(PASSES) - 1))
                        mm.then_inc(misc_done, 1)
                    elif kind == "QT":
                        pe.wait_ge(q_turned, it1 * UNITS + n + 1)
                        for h in range(GRP):
                            mm = nc.tensor.transpose(misc[:, h * P:(h + 1) * P], q_rot[:, h * P:(h + 1) * P], ident[:])
                        mm.then_inc(misc_done, 1)
                    elif kind == "S":
                        hd, W = n * GRP + j, (i + 1) * P
                        if j == 0:
                            pe.wait_ge(misc_empty, it1 * MPB + misc_no("QT", n) + 1)
                            if n % TB == 0:
                                pe.wait_ge(k_loaded[e % 2], (it1 + n // UNITS) * 16 + 16)
                        pe.wait_ge(exp_done, it1 * HPB + hd - 1)
                        sc = scores[hd % 2]
                        cuts = [(c, min(c + 512, W)) for c in range(0, W, 512)]
                        for x, y in PASSES:
                            for c0, c1 in cuts:
                                mm = nc.tensor.matmul(sc[:, c0:c1], qT[:, u, x, j * P:(j + 1) * P],
                                                      kT[:, e % 2, y, c0:c1], start=(x == HI and y == HI),
                                                      stop=(x == LO))
                            if (x, y) == (HI, HI):
                                nc.tensor.matmul(sc[:, W - P:W], identb[:], mask[:], start=False, stop=False)
                        mm.then_inc(s_done, 1)
                    elif kind == "T":
                        t = first_key_block(n) + j
                        if j == 0:
                            pe.wait_ge(normed, it1 * HPB + (n + 1) * GRP)
                        pe.wait_ge(pT_split, it1 * KEYB + t - 1)
                        for h in range(GRP):
                            mm = nc.tensor.transpose(ptb[t % 2][:, h * P:(h + 1) * P],
                                                     prob[:, u, h, j * P:(j + 1) * P], ident[:])
                        mm.then_inc(t_done, 1)
                    elif kind == "PV":
                        t = first_key_block(n) + j
                        if j == 0:
                            pe.wait_ge(o_split, it1 * UNITS + n)
                            if n % TB == 0:
                                pe.wait_ge(v_loaded[e % 2], (it1 + n // UNITS) * 16 + 16)
                        pe.wait_ge(pT_split, it1 * KEYB + t + 1)
                        for x, y in PASSES:
                            mm = nc.tensor.matmul(ob[:], v_sb[:, e % 2, x, j], pT[:, t % 4, y],
                                                  start=(j == 0 and (x, y) == (HI, HI)),
                                                  stop=(j == i and x == LO))
                        if j == i:
                            mm.then_inc(o_done, 1)
                    elif kind == "W":
                        pe.wait_ge(o_split, it1 * UNITS + n + 1)
                        for h in range(GRP):
                            if n % TB == 0:
                                pe.wait_ge(wo_split, (it1 * 2 + e) * GRP + h + 1)
                            for m, (x, w) in enumerate(PASSES):
                                mm = nc.tensor.matmul(misc[:], oT[:, u, x, h * P:(h + 1) * P], wo[:, w, h],
                                                      start=(h == 0 and m == 0),
                                                      stop=(h == GRP - 1 and m == len(PASSES) - 1))
                        mm.then_inc(misc_done, 1)

            first, body, last = cut(WHOLE)
            pe.wait_ge(const, 6)
            work(first, 1)
            with pe.Fori(0, BODIES - 1) as it:
                work(body, it + 1)
            work(last, BODIES - 2)


def build(nc, a, out):
    scr = {
        "xT": nc.dram_tensor("xT_parts", [B * TB, P, 2, KC, P], F32, kind="Internal").ap(),
        "k": nc.dram_tensor("k_parts", [KVH, P, 2, B * S], F32, kind="Internal").ap(),
        "v": nc.dram_tensor("v_parts", [KVH, P, 2, B * TB, DH], F32, kind="Internal").ap(),
        "ffn": nc.dram_tensor("ffn_out", [B * TB, P, D], F32, kind="Internal").ap(),
    }
    key_value_and_ffn(nc, a, scr, [])
    attention(nc, a, scr, out)


def kernel(L0_attn_hidden_states, L0_attn_Wq, L0_attn_Wkr, L0_attn_Wdk, L0_attn_Wupk, L0_attn_Wupv,
           L0_attn_Wo, L0_ffn_W_gate, L0_ffn_W_up, L0_ffn_W_down):
    import numpy as np
    import concourse.bacc as bacc
    from concourse.bass_utils import run_bass_kernel_spmd

    x, Wq, Wkr, Wdk, Wupk, Wupv, Wo, Wg, Wu, Wd = (np.asarray(v) for v in (
        L0_attn_hidden_states, L0_attn_Wq, L0_attn_Wkr, L0_attn_Wdk, L0_attn_Wupk, L0_attn_Wupv,
        L0_attn_Wo, L0_ffn_W_gate, L0_ffn_W_up, L0_ffn_W_down))

    def by_partition(wt, cols):
        k, n = wt.shape
        return wt.reshape(k // P, P, n // cols, cols).transpose(2, 1, 0, 3)

    gate, up = (by_partition(w.T, P).reshape(MB, P, C) for w in (Wg, Wu))
    inv_freq = 1.0 / 10000.0 ** (np.arange(0, DH, 2, dtype=np.float32) / DH)
    freqs = np.outer(np.arange(S, dtype=np.float32), inv_freq)
    cs = np.stack([np.cos(freqs), np.sin(freqs)], 1).astype(np.float32)
    scale = np.float32(1.0) / np.sqrt(np.float32(DH))
    arrays = {
        "x": x.reshape(CHUNKS, CT, P, D).transpose(0, 2, 1, 3),
        "wq": by_partition(Wq.T, GRP * DH),
        "wkr": by_partition(Wkr.T, 512)[0],
        "wdk": by_partition(Wdk.T, 512)[0],
        "wupk": by_partition(Wupk.T, 512)[0],
        "wupv": by_partition(Wupv.T, 512),
        "wo": Wo.T.reshape(KVH, GRP, DH, D).transpose(0, 2, 1, 3),
        "ffw": np.concatenate([gate, up, Wd.T.reshape(MB, P, D)], axis=2),
        "ktab": np.tile(cs[:, :, 0:RH].reshape(S // CHUNK, CT, P, 2, RH).transpose(0, 2, 1, 3, 4),
                        (B, 1, 1, 1, 1)),
        "qtab": (cs * scale).reshape(TB, P, 2, HALF).transpose(1, 0, 2, 3),
    }
    arrays = {k: np.ascontiguousarray(v) for k, v in arrays.items()}
    nc = bacc.Bacc("TRN2", target_bir_lowering=False, num_devices=1)
    a = {k: nc.dram_tensor(f"in_{k}", v.shape, mybir.dt.from_np(v.dtype), kind="ExternalInput").ap()
         for k, v in arrays.items()}
    out = nc.dram_tensor("out", [B, P, TB, D], F32, kind="ExternalOutput").ap()
    build(nc, a, out)
    r = run_bass_kernel_spmd(nc, [{f"in_{k}": v for k, v in arrays.items()}], core_ids=[0])
    return np.ascontiguousarray(r.results[0]["out"].transpose(0, 2, 1, 3)).reshape(B, S, D)
```
